# Optimizing a Trainium2 kernel written in Bass

```python
import numpy as np
import jax
import jax.numpy as jnp

def _softmax(x, axis=-1):
    return jax.nn.softmax(x, axis=axis)

def _gelu(x):
    return jax.nn.gelu(x, approximate=True)

def _silu(x):
    return jax.nn.silu(x)

def _sigmoid(x):
    return jax.nn.sigmoid(x)

def _layernorm(x, axis=-1, eps=1e-05):
    m = jnp.mean(x, axis=axis, keepdims=True)
    v = jnp.var(x, axis=axis, keepdims=True)
    return (x - m) / jnp.sqrt(v + eps)

def _scatter_add(tgt, idx, src, axis=0):
    return tgt.at[idx].add(src)

def _segment_sum(src, seg, n):
    return jax.ops.segment_sum(src, seg, n)
kernel_name = 'mk_metaformer_d1_conv_nchw256_r4_5e6be4'

def setup_inputs(seed: int=0):
    np.random.seed(seed)
    _w = jnp.asarray

    def _rec_inputs():
        import jax
        import jax.numpy as jnp
        _gk = jax.random.key(seed)
        x = 7.22e-05 + 1 * jax.random.normal(jax.random.fold_in(_gk, 1), (8, 64, 16, 16), jnp.float32)
        return x
    x = _rec_inputs()

    def _L0_conv_setup():
        import jax, jax.numpy as jnp
        import numpy as np
        from jax import lax
        DIM = 8
        EPS_ATT = 1e-15
        BN_EPS = 1e-05

        def _relu_linear_att(qkv):
            B, C, H, W = qkv.shape
            n_heads = C // (3 * DIM)
            t = qkv.reshape(B, n_heads, 3 * DIM, H * W).transpose(0, 1, 3, 2)
            q = jax.nn.relu(t[..., :DIM])
            k = jax.nn.relu(t[..., DIM:2 * DIM])
            v = t[..., 2 * DIM:]
            v = jnp.concatenate([v, jnp.ones(v.shape[:-1] + (1,), v.dtype)], axis=-1)
            kv = jnp.einsum('bhnd,bhne->bhde', k, v)
            out = jnp.einsum('bhnd,bhde->bhne', q, kv)
            out = out[..., :-1] / (out[..., -1:] + EPS_ATT)
            return out.transpose(0, 1, 3, 2).reshape(B, n_heads * DIM, H, W)
        key = jax.random.key(seed)
        ks = jax.random.split(key, 6)
        s = 0.05
        x = jax.random.normal(ks[0], (8, 64, 16, 16), dtype=jnp.float32)
        w_qkv = jax.random.normal(ks[1], (192, 64), dtype=jnp.float32) * s
        w_dw = jax.random.normal(ks[2], (192, 1, 5, 5), dtype=jnp.float32) * s
        w_pw = jax.random.normal(ks[3], (24, 8, 8), dtype=jnp.float32) * s
        w_proj = jax.random.normal(ks[4], (64, 128), dtype=jnp.float32) * s
        bn_gamma = jnp.ones((64,), dtype=jnp.float32)
        bn_beta = jnp.zeros((64,), dtype=jnp.float32)
        bn_mean = jnp.zeros((64,), dtype=jnp.float32)
        bn_var = jnp.ones((64,), dtype=jnp.float32)
        return {'x': x, 'w_qkv': w_qkv, 'w_dw': w_dw, 'w_pw': w_pw, 'w_proj': w_proj, 'bn_gamma': bn_gamma, 'bn_beta': bn_beta, 'bn_mean': bn_mean, 'bn_var': bn_var}
    _L0_conv_all = _L0_conv_setup()
    _L0_conv_in = {k: v for k, v in _L0_conv_all.items() if k in ('w_qkv', 'w_dw', 'w_pw', 'w_proj', 'bn_gamma', 'bn_beta', 'bn_mean', 'bn_var')}
    del _L0_conv_all

    def _L0_ffn_setup():
        import jax, jax.numpy as jnp
        import numpy as np
        TOP_K = 2
        key = jax.random.key(seed)
        ks = jax.random.split(key, 4)
        B, L, D, H, E = (8, 1024, 64, 256, 8)
        s = 0.02
        return {'x': jax.random.normal(ks[0], (B, L, D), jnp.float32), 'Wg': jax.random.normal(ks[1], (D, E), jnp.float32) * s, 'bg': jnp.zeros((E,), jnp.float32), 'W1': jax.random.normal(ks[2], (E, D, H), jnp.float32) * s, 'b1': jnp.zeros((E, H), jnp.float32), 'W2': jax.random.normal(ks[3], (E, H, D), jnp.float32) * s, 'b2': jnp.zeros((E, D), jnp.float32)}
    _L0_ffn_all = _L0_ffn_setup()
    _L0_ffn_in = {k: v for k, v in _L0_ffn_all.items() if k in ('Wg', 'bg', 'W1', 'b1', 'W2', 'b2')}
    del _L0_ffn_all
    return {'x': x, 'L0_conv_w_qkv': _L0_conv_in['w_qkv'], 'L0_conv_w_dw': _L0_conv_in['w_dw'], 'L0_conv_w_pw': _L0_conv_in['w_pw'], 'L0_conv_w_proj': _L0_conv_in['w_proj'], 'L0_conv_bn_gamma': _L0_conv_in['bn_gamma'], 'L0_conv_bn_beta': _L0_conv_in['bn_beta'], 'L0_conv_bn_mean': _L0_conv_in['bn_mean'], 'L0_conv_bn_var': _L0_conv_in['bn_var'], 'L0_ffn_Wg': _L0_ffn_in['Wg'], 'L0_ffn_bg': _L0_ffn_in['bg'], 'L0_ffn_W1': _L0_ffn_in['W1'], 'L0_ffn_b1': _L0_ffn_in['b1'], 'L0_ffn_W2': _L0_ffn_in['W2'], 'L0_ffn_b2': _L0_ffn_in['b2']}

def reference(x, L0_conv_w_qkv, L0_conv_w_dw, L0_conv_w_pw, L0_conv_w_proj, L0_conv_bn_gamma, L0_conv_bn_beta, L0_conv_bn_mean, L0_conv_bn_var, L0_ffn_Wg, L0_ffn_bg, L0_ffn_W1, L0_ffn_b1, L0_ffn_W2, L0_ffn_b2):
    import jax
    import jax.numpy as jnp

    def _L0_conv_ref(x, w_qkv, w_dw, w_pw, w_proj, bn_gamma, bn_beta, bn_mean, bn_var):
        import jax, jax.numpy as jnp
        import numpy as np
        from jax import lax
        DIM = 8
        EPS_ATT = 1e-15
        BN_EPS = 1e-05

        def _relu_linear_att(qkv):
            B, C, H, W = qkv.shape
            n_heads = C // (3 * DIM)
            t = qkv.reshape(B, n_heads, 3 * DIM, H * W).transpose(0, 1, 3, 2)
            q = jax.nn.relu(t[..., :DIM])
            k = jax.nn.relu(t[..., DIM:2 * DIM])
            v = t[..., 2 * DIM:]
            v = jnp.concatenate([v, jnp.ones(v.shape[:-1] + (1,), v.dtype)], axis=-1)
            kv = jnp.einsum('bhnd,bhne->bhde', k, v)
            out = jnp.einsum('bhnd,bhde->bhne', q, kv)
            out = out[..., :-1] / (out[..., -1:] + EPS_ATT)
            return out.transpose(0, 1, 3, 2).reshape(B, n_heads * DIM, H, W)
        B, _, H, W = x.shape
        qkv = jnp.einsum('bchw,oc->bohw', x, w_qkv)
        C3 = qkv.shape[1]
        dw = lax.conv_general_dilated(qkv, w_dw, window_strides=(1, 1), padding=[(2, 2), (2, 2)], feature_group_count=C3, dimension_numbers=('NCHW', 'OIHW', 'NCHW'))
        G = w_pw.shape[0]
        pw = jnp.einsum('bgihw,goi->bgohw', dw.reshape(B, G, C3 // G, H, W), w_pw)
        pw = pw.reshape(B, C3, H, W)
        ms = jnp.concatenate([qkv, pw], axis=1)
        att = _relu_linear_att(ms)
        out = jnp.einsum('bchw,oc->bohw', att, w_proj)
        inv = bn_gamma / jnp.sqrt(bn_var + BN_EPS)
        out = out * inv[None, :, None, None] + (bn_beta - bn_mean * inv)[None, :, None, None]
        return out

    def _L0_ffn_ref(x, Wg, bg, W1, b1, W2, b2):
        import jax, jax.numpy as jnp
        import numpy as np
        TOP_K = 2
        B, L, D = x.shape
        E = W1.shape[0]
        xf = x.reshape(-1, D)
        gate_logits = xf @ Wg + bg
        top_w, top_i = jax.lax.top_k(gate_logits, TOP_K)
        top_w = jax.nn.softmax(top_w, axis=-1)
        w_dense = jnp.sum(jax.nn.one_hot(top_i, E, dtype=xf.dtype) * top_w[..., None], axis=1)
        out = jnp.zeros_like(xf)
        for e in range(E):
            h = jax.nn.gelu(xf @ W1[e] + b1[e], approximate=False)
            out = out + w_dense[:, e:e + 1] * (h @ W2[e] + b2[e])
        return out.reshape(B, L, D)

    def _gn(v, G=32, eps=1e-05):
        B_, C_, H_, W_ = v.shape
        g = v.reshape(B_, G, C_ // G, H_, W_)
        m = jnp.mean(g, axis=(2, 3, 4), keepdims=True)
        s = jnp.var(g, axis=(2, 3, 4), keepdims=True)
        return ((g - m) / jnp.sqrt(s + eps)).reshape(v.shape)

    def _ln_c(v, eps=1e-06):
        m = jnp.mean(v, axis=1, keepdims=True)
        s = jnp.var(v, axis=1, keepdims=True)
        return (v - m) / jnp.sqrt(s + eps)

    def _ln_t(v, eps=1e-05):
        m = jnp.mean(v, axis=-1, keepdims=True)
        s = jnp.var(v, axis=-1, keepdims=True)
        return (v - m) / jnp.sqrt(s + eps)

    def _to_tokens(v):
        B_, C_, H_, W_ = v.shape
        return v.reshape(B_, C_, H_ * W_).transpose(0, 2, 1)

    def _from_tokens(t, like):
        B_, C_, H_, W_ = like.shape
        return t.transpose(0, 2, 1).reshape(B_, C_, H_, W_)
    x = x + _L0_conv_ref(_ln_c(x), L0_conv_w_qkv, L0_conv_w_dw, L0_conv_w_pw, L0_conv_w_proj, L0_conv_bn_gamma, L0_conv_bn_beta, L0_conv_bn_mean, L0_conv_bn_var)
    t = _to_tokens(x)
    t = t + _L0_ffn_ref(_ln_t(t), L0_ffn_Wg, L0_ffn_bg, L0_ffn_W1, L0_ffn_b1, L0_ffn_W2, L0_ffn_b2)
    x = _from_tokens(t, x)
    return x

_drawn_inputs = setup_inputs


def setup_inputs(seed=0):
    import zlib

    import numpy as np

    out = dict(_drawn_inputs(seed))
    spreads = {'L0_conv_bn_gamma': (1.0, 0.6),
     'L0_conv_bn_beta': (0.0, 0.1),
     'L0_conv_bn_mean': (0.0, 0.1),
     'L0_conv_bn_var': (1.0, 0.6),
     'L0_ffn_bg': (0.0, 0.1),
     'L0_ffn_b1': (0.0, 0.674),
     'L0_ffn_b2': (0.0, 0.1)}
    factors = {'L0_conv_w_dw': 8.0, 'L0_conv_w_pw': 8.0, 'L0_ffn_W1': 3.048}
    for name, (base, spread) in spreads.items():
        noise = np.random.default_rng([zlib.crc32(name.encode()), seed]).standard_normal(out[name].shape)
        drawn = base * np.exp(spread * noise) if base else spread * noise
        out[name] = jnp.asarray(drawn.astype(out[name].dtype))
    for name, factor in factors.items():
        out[name] = (out[name] * factor).astype(out[name].dtype)
    return out
```

```python
from contextlib import ExitStack

import concourse.bass as bass
from concourse import mybir
import numpy as np

F32 = mybir.dt.float32
F32R = mybir.dt.float32r
ALU = mybir.AluOpType
ACT = mybir.ActivationFunctionType
AX = mybir.AxisListType

B, C, H, W = 8, 64, 16, 16
N = H * W
G, I = 24, 8
QKV = G * I
DY = DX = 5
PAD = DY // 2
YP = H + 2 * PAD
HEADS = 16
HD = HEADS * I
MSW = 3 * HD + 1
KW = HD + 1
NW = HD + HEADS
E, HID, KC = 8, 256, 2
PAIRS = B // 2
TILES = 4
PT = TILES * 128
LN_C_EPS, LN_T_EPS, BN_EPS, ATT_EPS = 1e-6, 1e-5, 1e-5, 1e-15

C_CENTER, C_ONES = 0, 128
C_IDENT = C_ONES + 2
C_HEAD = C_IDENT + 128
C_PAR = C_HEAD + HEADS
C_REV = C_PAR + 2
C_END = C_REV + E
SELW = (2 * W - 1) * I


def constants():
    c = np.zeros((128, C_END), np.float32)
    p = np.arange(128)
    half = p // C
    same = half[:, None] == half[None, :]
    c[:, C_CENTER:C_CENTER + 128] = np.eye(128) - same / C
    c[:, C_ONES:C_ONES + 2] = (half[:, None] == np.arange(2)) / C
    c[:, C_IDENT:C_IDENT + 128] = np.eye(128)
    c[:, C_HEAD:C_HEAD + HEADS] = (p // I)[:, None] == np.arange(HEADS)
    c[:, C_PAR:C_PAR + 2] = ((p // H) % 2)[:, None] == np.arange(2)
    c[:, C_REV:C_REV + E] = E - np.arange(E)
    s = np.zeros((DX, I, 2 * W - 1, I), np.float32)
    for dx in range(DX):
        for i in range(I):
            s[dx, i, dx - PAD + W - 1, i] = 1
    return c, s.reshape(DX * I, SELW)


def build(nc, x, w_qkv, w_dw, w_pw, w_proj, vectors, wg, w1, b1, w2, b2, consts, select, out):
    ctx = ExitStack()
    with ctx:
        def sb(name, shape, dt=F32):
            return ctx.enter_context(nc.sbuf_tensor(name, shape, dt))

        def sem(name):
            return ctx.enter_context(nc.semaphore(name))

        X = sb("X", [128, 4 * N])
        CST = sb("CST", [128, C_END])
        SEL = sb("SEL", [DX * I, SELW])
        WD = sb("WD", [DX * I, G * DY])
        PW = sb("PW", [128, G, I])
        WQ = sb("WQ", [128, 2 * QKV])
        WP = sb("WP", [128, C])
        VEC = sb("VEC", [128, 4 * C + E])
        WG = sb("WG", [128, E])
        W1 = sb("W1", [128, E * HID])
        B1 = sb("B1", [128, E * KC])
        W2 = sb("W2", [128, E * KC, C])
        B2 = sb("B2", [TILES * E, TILES * C])
        INV = sb("INV", [128, 2, C])
        BIAS = sb("BIAS", [128, C])
        HALF = sb("HALF", [128, C + 16])
        EULER = sb("EULER", [128, TILES])
        WPS = sb("WPS", [128, C])
        WGH, WGL = sb("WGH", [128, E], F32R), sb("WGL", [128, E], F32R)
        W1H, W1L = sb("W1H", [128, E * HID], F32R), sb("W1L", [128, E * HID], F32R)
        RS = sb("RS", [128, G, DY, W])
        BAND = sb("BAND", [128, G * DY * 128])
        XC = sb("XC", [128, 4 * N])
        SQ = sb("SQ", [128, 4 * N])
        VAR1 = sb("VAR1", [128, 8, 2])
        R1 = sb("R1", [128, 8, 2])
        MS = sb("MS", [128, 16, MSW])
        QP = sb("QP", [128, G, YP * B])
        XB = sb("XB", [128, 16, C])
        KM = sb("KM", [128, 2, 2, 4, HD])
        KV = sb("KV", [128, 2, 2, NW])
        QT = sb("QT", [128, 2, 2, N])
        DEN = sb("DEN", [128, 2, TILES, HEADS])
        ATT = sb("ATT", [128, TILES, HD])
        ATTT = sb("ATTT", [128, PT])
        X2 = sb("X2", [128, 2, TILES, C])
        XC2 = sb("XC2", [128, TILES, C])
        SQ2 = sb("SQ2", [128, TILES, C])
        SM = sb("SM", [128, 4, TILES])
        XH2 = sb("XH2", [128, TILES, 2, C])
        XS = sb("XS", [128, 2, PT], F32R)
        TOP = sb("TOP", [128, 8, TILES, E])
        TS = sb("TS", [128, 8, TILES])
        WDN = sb("WDN", [128, 2, TILES, E])
        WDT = sb("WDT", [TILES * E, 128])
        PROD = sb("PROD", [128, 8, C])
        RED = sb("RED", [128, 2, TILES, C])
        FIN = sb("FIN", [128, 2, TILES, C])

        band = BAND[:, :].rearrange("p (g d m) -> p g d m", g=G, d=DY)
        HRING = 4
        hidden = BAND[:, 0:HRING * PT].rearrange("p (r t) -> p r t", r=HRING)
        outs = BAND[0:C, HRING * PT:HRING * PT + PAIRS * PT].rearrange("c (s t) -> c s t", s=PAIRS)
        CEN = CST[:, C_CENTER:C_CENTER + 128]
        ONES = CST[:, C_ONES:C_ONES + 2]
        IDT = CST[:, C_IDENT:C_IDENT + 128]
        PAR = CST[:, C_PAR:C_PAR + 2]

        PS = ctx.enter_context(nc.psum_tensor("PS", [128, 8, 512], F32))
        CENTER_BANKS, VAR_BANK = (0, 1), 2
        RS_BANK0 = 3
        QKV_RING = (7, 0, 1, 2)
        XT_BANKS = (3, 4)
        CONV_RING = (5, 6, 7, 0)
        Y_BANK0 = 0
        H_RING = (4, 5)
        A, Bk = 6, 7

        x_in, cst_in, sel_in, pw_in, wq_in = sem("x_in"), sem("cst_in"), sem("sel_in"), sem("pw_in"), sem("wq_in")
        vec_in, w1_in, w2_in = sem("vec_in"), sem("w1_in"), sem("w2_in")
        wq_zero, b2_zero = sem("wq_zero"), sem("b2_zero")
        consts_set = sem("consts_set")
        rs_ready, rs_copied = sem("rs_ready"), sem("rs_copied")
        centred, xc_ready, sq_ready = sem("centred"), sem("xc_ready"), sem("sq_ready")
        var_ready, var_guarded, r1_ready = sem("var_ready"), sem("var_guarded"), sem("r1_ready")
        qkv_ready, qkv_scaled = sem("qkv_ready"), sem("qkv_scaled")
        qp_ready = sem("qp_ready")
        band_v, band_p = sem("band_v"), sem("band_p")
        conv_ready, conv_moved = sem("conv_ready"), sem("conv_moved")
        xt_ready, xb_ready = sem("xt_ready"), sem("xb_ready")
        inv_ready, bias_ready, wps_ready = sem("inv_ready"), sem("bias_ready"), sem("wps_ready")
        w_high, w_low = sem("w_high"), sem("w_low")
        a_filled, a_read, b_filled, b_read = sem("a_filled"), sem("a_read"), sem("b_filled"), sem("b_read")
        km_ready = sem("km_ready")
        v2_ready, r2_ready, xh_ready = sem("v2_ready"), sem("r2_ready"), sem("xh_ready")
        hi_ready = sem("hi_ready")
        gap_ready, exp_ready, wdn_ready = sem("gap_ready"), sem("exp_ready"), sem("wdn_ready")
        h_ready, gelu_done, y_read = sem("h_ready"), sem("gelu_done"), sem("y_read")
        w2_done = sem("w2_done")
        fin_ready, stored = sem("fin_ready"), sem("stored")
        v_chain, p_chain = sem("v_chain"), sem("p_chain")

        a_uses, b_uses = {}, {}
        for s in range(-1, PAIRS):
            if s >= 0:
                b_uses["gate", s] = len(b_uses)
            if s + 1 < PAIRS:
                a_uses["kv", s + 1] = len(a_uses)
                b_uses["qt", s + 1] = len(b_uses)
                a_uses["num", s + 1] = len(a_uses)
                b_uses["num", s + 1] = len(b_uses)
            if s >= 0:
                b_uses["wdt", s] = len(b_uses)
                if s >= 1:
                    a_uses["fin", s - 1] = len(a_uses)
                b_uses["b2", s] = len(b_uses)
            if s + 1 < PAIRS:
                a_uses["attt", s + 1] = len(a_uses)
                b_uses["proj", s + 1] = len(b_uses)
                a_uses["xt", s + 1] = len(a_uses)
        a_uses["fin", PAIRS - 1] = len(a_uses)

        def by_pixel(k):
            return PS[:, CENTER_BANKS[k], :].rearrange("p (t q r) -> p r q t", q=4, r=4)

        def pair_tokens(t, k):
            return t[:, 512 * k:512 * k + 512].rearrange("p (r q t) -> p r q t", q=4, r=4)

        block = ctx.enter_context(nc.Block())

        @block.sync
        def _(sp):
            xs = x.rearrange("(h b) c y x -> h c b (y x)", h=2)
            for h in range(2):
                sp.dma_start(X[C * h:C * h + C, :].rearrange("c (b n) -> c b n", b=4), xs[h]).then_inc(x_in, 16)
            sp.wait_ge(wq_zero, 1)
            for h in range(2):
                sp.dma_start(WQ[C * h:C * h + C, QKV * h:QKV * h + QKV], w_qkv).then_inc(wq_in, 16)
            sp.dma_start(VEC[:, :], vectors.unsqueeze(0).broadcast_to([128, 4 * C + E])).then_inc(vec_in, 16)
            sp.dma_start(WP[:, :], w_proj).then_inc(vec_in, 16)
            for h in range(2):
                sp.dma_start(WG[C * h:C * h + C, :], wg).then_inc(w1_in, 16)
                sp.dma_start(W1[C * h:C * h + C, :].rearrange("c (e n) -> c e n", e=E),
                             w1.rearrange("e c n -> c e n")).then_inc(w1_in, 16)
            for s in range(PAIRS):
                sp.wait_ge(a_read, a_uses["fin", s] + 1)
                sp.dma_start(out[2 * s:2 * s + 2].rearrange("b c y x -> c b (y x)"),
                             outs[:, s, :].rearrange("c (b n) -> c b n", b=2)).then_inc(stored, 16)
            sp.wait_ge(stored, 16 * PAIRS)

        @block.gpsimd
        def _(pool):
            pool.memset(WQ[:, :], 0.0).then_inc(wq_zero, 1)
            pool.memset(B2[:, :], 0.0).then_inc(b2_zero, 1)
            pool.memset(HALF[:, :], -0.5).then_inc(consts_set, 1)
            pool.memset(EULER[:, :], float(np.e)).then_inc(consts_set, 1)
            pool.memset(QP[:, :, 0:PAD * B], 0.0).then_inc(consts_set, 1)
            pool.memset(QP[:, :, (PAD + H) * B:YP * B], 0.0).then_inc(consts_set, 1)
            pool.memset(MS[:, :, 3 * HD:MSW], 1.0).then_inc(consts_set, 1)
            pool.wait_ge(consts_set, 5)
            pool.wait_ge(vec_in, 32)
            pool.tensor_scalar(INV[:, 0, :], VEC[:, 3 * C:4 * C], 1.0, BN_EPS, ALU.mult, ALU.add).then_inc(p_chain, 1)
            pool.wait_ge(p_chain, 1)
            pool.tensor_tensor(INV[:, 1, :], INV[:, 0, :], HALF[:, 0:C], ALU.pow).then_inc(inv_ready, 1)
            pool.wait_ge(var_guarded, 1)
            pool.tensor_tensor(R1[:, :, :].rearrange("p j h -> p (j h)"),
                               VAR1[:, :, :].rearrange("p j h -> p (j h)"), HALF[:, 0:16], ALU.pow).then_inc(r1_ready, 1)
            pool.wait_ge(rs_copied, 4)
            pool.wait_ge(pw_in, 16)
            for g in range(2, G, 3):
                pool.tensor_tensor(
                    band[:, g].rearrange("p d (x o) -> p (d x) o", o=I),
                    RS[:, g].rearrange("p d x -> p (d x)").unsqueeze(2).broadcast_to([128, DY * W, I]),
                    PW[:, g, :].unsqueeze(1).broadcast_to([128, DY * W, I]), ALU.mult).then_inc(band_p, 1)
            pool.wait_ge(w_high, 2)
            pool.tensor_tensor(W1L[:, :], W1[:, :], W1H[:, :].bitcast(F32), ALU.subtract).then_inc(w_low, 1)
            pool.tensor_tensor(WGL[:, :], WG[:, :], WGH[:, :].bitcast(F32), ALU.subtract).then_inc(w_low, 1)
            n = 1

            def pow_r2():
                nonlocal n
                pool.wait_ge(v2_ready, pow_r2.s + 1)
                pool.tensor_scalar(SM[:, 2, :], SM[:, 1, :], 1.0 / C, LN_T_EPS, ALU.mult, ALU.add).then_inc(p_chain, 1)
                n += 1
                pool.wait_ge(p_chain, n)
                pool.tensor_tensor(SM[:, 3, :], SM[:, 2, :], HALF[:, 0:TILES], ALU.pow).then_inc(r2_ready, 1)
                pow_r2.s += 1
            pow_r2.s = 0
            pow_r2()
            for s in range(PAIRS):
                pool.wait_ge(gap_ready, s + 1)
                pool.tensor_tensor(TS[:, 5, :], EULER[:, :], TS[:, 4, :], ALU.pow).then_inc(exp_ready, 1)
                if s + 1 < PAIRS:
                    pow_r2()

        @block.scalar
        def _(act):
            act.dma_start(SEL[:, :], select).then_inc(sel_in, 16)
            act.dma_start(WD[:, :], w_dw).then_inc(sel_in, 16)
            act.dma_start(CST[:, :], consts).then_inc(cst_in, 16)
            act.dma_start(PW[:, :, :].rearrange("p g o -> p (g o)"),
                          w_pw.unsqueeze(0).broadcast_to([W, I, QKV])).then_inc(pw_in, 16)
            act.dma_start(W2[:, :, :].rearrange("p k c -> p (k c)"), w2).then_inc(w2_in, 16)
            act.dma_start(B1[:, :], b1).then_inc(w2_in, 16)
            act.wait_ge(b2_zero, 1)
            for t in range(TILES):
                act.dma_start(B2[E * t:E * t + E, C * t:C * t + C], b2).then_inc(w2_in, 16)
            for k in range(4):
                act.wait_ge(rs_ready, k + 1)
                act.activation(RS[:, :, :, 4 * k:4 * k + 4].rearrange("p g d x -> p (g d) x"),
                               PS[:, RS_BANK0 + k, 0:480].rearrange("p (x m) -> p m x", x=4),
                               ACT.Copy).then_inc(rs_copied, 1)
            for k in range(2):
                act.wait_ge(centred, k + 1)
                act.activation(pair_tokens(SQ, k), by_pixel(k), ACT.Square).then_inc(sq_ready, 1)
            act.wait_ge(w1_in, 64)
            act.activation(W1H[:, :], W1[:, :], ACT.Copy).then_inc(w_high, 1)
            act.activation(WGH[:, :], WG[:, :], ACT.Copy).then_inc(w_high, 1)

            def relu_qt(s):
                act.wait_ge(b_filled, b_uses["qt", s] + 1)
                if s >= 2:
                    act.wait_ge(b_filled, b_uses["num", s - 2] + 1)
                for b2i in range(2):
                    i = act.activation(
                        QT[:, s % 2, b2i, :].rearrange("p (y q r) -> p r q y", q=4, r=4),
                        PS[:, Bk, :].rearrange("p (r q b y) -> p b r q y", r=4, q=4, b=2)[:, b2i],
                        ACT.Relu)
                i.then_inc(b_read, 1)

            def copy_attt(s):
                act.wait_ge(a_filled, a_uses["attt", s] + 1)
                if s >= 1:
                    act.wait_ge(b_filled, b_uses["proj", s - 1] + 1)
                act.activation(ATTT[:, :], PS[:, A, :], ACT.Copy).then_inc(a_read, 1)

            def high_xs(s):
                act.wait_ge(a_filled, a_uses["xt", s] + 1)
                if s >= 2:
                    act.wait_ge(h_ready, 16 * (s - 1))
                act.activation(XS[:, s % 2, :], PS[:, A, :], ACT.Copy).then_inc(hi_ready, 1)

            def copy_wdt(s):
                act.wait_ge(b_filled, b_uses["wdt", s] + 1)
                if s >= 1:
                    act.wait_ge(b_filled, b_uses["b2", s - 1] + 1)
                act.activation(WDT[:, :], PS[0:TILES * E, Bk, 0:128], ACT.Copy).then_inc(b_read, 1)

            def copy_out(s):
                act.wait_ge(a_filled, a_uses["fin", s] + 1)
                act.activation(outs[:, s, :], PS[0:C, A, :], ACT.Copy).then_inc(a_read, 1)

            relu_qt(0)
            copy_attt(0)
            high_xs(0)
            for s in range(PAIRS):
                for e in range(E):
                    for k in range(KC * e, KC * e + KC):
                        n = KC * E * s + k
                        act.wait_ge(h_ready, n + 1)
                        if n >= HRING:
                            act.wait_ge(w2_done, n // KC - 1)
                        act.activation(hidden[:, n % HRING, :], PS[:, H_RING[n % 2], :], ACT.Gelu,
                                       bias=B1[:, k:k + 1]).then_inc(gelu_done, 1)
                    if e == 1 and s + 1 < PAIRS:
                        relu_qt(s + 1)
                    if e == 3:
                        copy_wdt(s)
                        if s >= 1:
                            copy_out(s - 1)
                    if e == 4 and s + 1 < PAIRS:
                        copy_attt(s + 1)
                    if e == 7 and s + 1 < PAIRS:
                        high_xs(s + 1)
            copy_out(PAIRS - 1)

        @block.vector
        def _(dve):
            chain = [0]

            def link(i):
                chain[0] += 1
                i.then_inc(v_chain, 1)
                dve.wait_ge(v_chain, chain[0])

            def bands(g):
                dve.tensor_tensor(
                    band[:, g].rearrange("p d (x o) -> p (d x) o", o=I),
                    RS[:, g].rearrange("p d x -> p (d x)").unsqueeze(2).broadcast_to([128, DY * W, I]),
                    PW[:, g, :].unsqueeze(1).broadcast_to([128, DY * W, I]), ALU.mult).then_inc(band_v, 1)

            for k in range(2):
                dve.wait_ge(centred, k + 1)
                dve.wait_ge(sq_ready, k + 1)
                dve.tensor_copy(pair_tokens(XC, k), by_pixel(k)).then_inc(xc_ready, 1)
            dve.wait_ge(var_ready, 1)
            dve.tensor_scalar(VAR1[:, :, :].rearrange("p j h -> p (j h)"), PS[:, VAR_BANK, 0:16],
                              LN_C_EPS, None, ALU.add).then_inc(var_guarded, 1)
            dve.wait_ge(rs_copied, 4)
            dve.wait_ge(pw_in, 16)
            bands(0)
            bands(1)
            dve.wait_ge(r1_ready, 1)
            for j in range(8):
                dve.wait_ge(qkv_ready, j + 1)
                sp_, xr = divmod(j, 4)
                for h in range(2):
                    i = dve.tensor_scalar(
                        MS[:, 4 * (2 * h + sp_) + xr, 0:3 * HD].rearrange("p (q h i) -> p h q i", q=3, i=I)[:, 0:8],
                        PS[:, QKV_RING[j % 4], QKV * h:QKV * h + QKV].rearrange("p (h q i) -> p h q i", q=3, i=I),
                        R1[:, j, h:h + 1], None, ALU.mult)
                i.then_inc(qkv_scaled, 1)
            dve.wait_ge(qkv_scaled, 8)
            dve.wait_ge(consts_set, 5)

            def head(h):
                return MS[:, :, 0:3 * HD].rearrange("p j (q h i) -> p h q j i", q=3, i=I)[:, h]

            qp = QP[:, :, :].rearrange("p g (y b) -> p g b y", b=B)
            for h in range(8):
                dve.transpose(qp[:, 3 * h:3 * h + 3, :, PAD:PAD + H],
                              head(h)).then_inc(qp_ready, 1)
                if h >= 1:
                    bands(3 * h)
                    bands(3 * h + 1)
                if h == 2:
                    dve.wait_ge(inv_ready, 1)
                    link(dve.tensor_tensor(INV[:, 0, :], INV[:, 1, :], VEC[:, 0:C], ALU.mult))
                    dve.tensor_tensor(WPS[:, :], WP[:, :], INV[:, 0, :], ALU.mult).then_inc(wps_ready, 1)
                    link(dve.tensor_tensor(BIAS[:, :], VEC[:, 2 * C:3 * C], INV[:, 0, :], ALU.mult))
                    link(dve.tensor_tensor(BIAS[:, :], VEC[:, C:2 * C], BIAS[:, :], ALU.subtract))
                if h == 3:
                    for k in range(2):
                        dve.wait_ge(xt_ready, k + 1)
                        dve.tensor_tensor(
                            XB[:, :, :].rearrange("p (h t) c -> p t h c", h=2)[:, 4 * k:4 * k + 4],
                            PS[:, XT_BANKS[k], :].rearrange("p (t h c) -> p t h c", t=4, h=2),
                            BIAS[:, :].unsqueeze(1).unsqueeze(1).broadcast_to([128, 4, 2, C]),
                            ALU.add).then_inc(xb_ready, 1)
            for h in range(8):
                dve.wait_ge(conv_ready, h + 1)
                dve.transpose(
                    head(8 + h),
                    PS[:, CONV_RING[h % 4], 0:3 * 128].rearrange("p (q y b) -> p q b y", q=3, b=B)).then_inc(conv_moved, 1)

            def mask_k(s):
                if s >= 2:
                    dve.wait_ge(a_filled, a_uses["kv", s - 2] + 1)
                for b in range(2):
                    dve.tensor_scalar(
                        KM[:, s % 2, b, :, :], MS[:, 4 * s:4 * s + 4, HD:2 * HD],
                        0.0, PAR[:, b:b + 1], ALU.max, ALU.mult).then_inc(km_ready, 1)

            def read_kv(s):
                dve.wait_ge(a_filled, a_uses["kv", s] + 1)
                kv = PS[:, A, 0:2 * KW].rearrange("p (b v) -> p b v", b=2)
                own = CST[:, C_HEAD:C_HEAD + HEADS].unsqueeze(1)
                dve.tensor_tensor(KV[:, s % 2, :, 0:HD].rearrange("p b (h v) -> p b h v", v=I),
                                  kv[:, :, 0:HD].rearrange("p b (h v) -> p b h v", v=I),
                                  own.unsqueeze(3).broadcast_to([128, 2, HEADS, I]), ALU.mult)
                dve.tensor_tensor(KV[:, s % 2, :, HD:NW], kv[:, :, HD:KW].broadcast_to([128, 2, HEADS]),
                                  own.broadcast_to([128, 2, HEADS]), ALU.mult).then_inc(a_read, 1)

            def attend(s):
                dve.wait_ge(a_filled, a_uses["num", s] + 1)
                dve.wait_ge(b_filled, b_uses["num", s] + 1)
                nd = PS[:, A:A + 2, 0:2 * NW].rearrange("p k (t v) -> p k t v", t=2)
                link(dve.tensor_scalar(DEN[:, 0, :, :].rearrange("p (k t) h -> p k t h", k=2), nd[:, :, :, HD:NW],
                                       ATT_EPS, None, ALU.add))
                link(dve.reciprocal(DEN[:, 1, :, :].rearrange("p t h -> p (t h)"),
                                    DEN[:, 0, :, :].rearrange("p t h -> p (t h)")))
                if s >= 1:
                    dve.wait_ge(a_filled, a_uses["attt", s - 1] + 1)
                for k, read in enumerate((a_read, b_read)):
                    i = dve.tensor_tensor(
                        ATT[:, 2 * k:2 * k + 2, :].rearrange("p t (h v) -> p t h v", v=I),
                        nd[:, k, :, 0:HD].rearrange("p t (h v) -> p t h v", v=I),
                        DEN[:, 1, 2 * k:2 * k + 2, :].unsqueeze(3).broadcast_to([128, 2, HEADS, I]), ALU.mult)
                    i.then_inc(read, 1)

            def norm(s):
                dve.wait_ge(b_filled, b_uses["proj", s] + 1)
                x2 = X2[:, s % 2]
                dve.tensor_tensor(x2, PS[:, Bk, 0:TILES * C].rearrange("p (t c) -> p t c", t=TILES),
                                  XB[:, TILES * s:TILES * s + TILES, :], ALU.add).then_inc(b_read, 1)
                dve.wait_ge(b_read, b_uses["proj", s] + 1)
                link(dve.tensor_reduce(SM[:, 0, :], x2, AX.X, ALU.add))
                link(dve.scalar_tensor_tensor(out=XC2[:, :, :], in0=SM[:, 0, :].unsqueeze(2).broadcast_to([128, TILES, C]),
                                              scalar=-1.0 / C, in1=x2, op0=ALU.mult, op1=ALU.add))
                link(dve.tensor_tensor(SQ2[:, :, :], XC2[:, :, :], XC2[:, :, :], ALU.mult))
                dve.tensor_reduce(SM[:, 1, :], SQ2[:, :, :], AX.X, ALU.add).then_inc(v2_ready, 1)

            def scale(s):
                dve.wait_ge(r2_ready, s + 1)
                if s >= 1:
                    dve.wait_ge(a_filled, a_uses["xt", s - 1] + 1)
                dve.tensor_tensor(XH2[:, :, :, :], XC2[:, :, :].unsqueeze(2).broadcast_to([128, TILES, 2, C]),
                                  SM[:, 3, :].unsqueeze(2).unsqueeze(3).broadcast_to([128, TILES, 2, C]),
                                  ALU.mult).then_inc(xh_ready, 1)

            def low_xs(s):
                dve.wait_ge(hi_ready, s + 1)
                dve.tensor_tensor(XS[C:2 * C, s % 2, :], PS[C:2 * C, A, :], XS[C:2 * C, s % 2, :].bitcast(F32),
                                  ALU.subtract).then_inc(a_read, 1)

            def top2(s):
                L, E1, C1, O1, L2, O2 = (TOP[:, k] for k in range(6))
                m1, r, m2, r2_, gap, ex, dn = (TS[:, k] for k in range(7))
                w1_ = TS[:, 7]

                def wide(v):
                    return v.unsqueeze(2).broadcast_to([128, TILES, E])

                def rows(v):
                    return v.unsqueeze(1).broadcast_to([128, TILES, E])

                rev = rows(CST[:, C_REV:C_REV + E])
                dve.wait_ge(b_filled, b_uses["gate", s] + 1)
                dve.tensor_tensor(L, PS[:, Bk, 0:TILES * E].rearrange("p (t e) -> p t e", t=TILES),
                                  rows(VEC[:, 4 * C:4 * C + E]), ALU.add).then_inc(b_read, 1)
                dve.wait_ge(b_read, b_uses["gate", s] + 1)
                for lg, m, o in ((L, m1, O1), (L2, m2, O2)):
                    link(dve.tensor_reduce(m, lg, AX.X, ALU.max))
                    link(dve.tensor_tensor(E1, lg, wide(m), ALU.is_equal))
                    link(dve.tensor_tensor(C1, E1, rev, ALU.mult))
                    link(dve.tensor_reduce(r, C1, AX.X, ALU.max))
                    link(dve.tensor_tensor(o, C1, wide(r), ALU.is_equal))
                    if o is O1:
                        link(dve.scalar_tensor_tensor(out=L2, in0=O1, scalar=-3e38, in1=L, op0=ALU.mult, op1=ALU.add))
                dve.tensor_tensor(gap, m2, m1, ALU.subtract).then_inc(gap_ready, 1)
                dve.wait_ge(exp_ready, s + 1)
                link(dve.tensor_scalar(dn, ex, 1.0, None, ALU.add))
                link(dve.reciprocal(w1_, dn))
                link(dve.tensor_tensor(r2_, ex, w1_, ALU.mult))
                link(dve.tensor_tensor(O1, O1, wide(w1_), ALU.mult))
                link(dve.tensor_tensor(O2, O2, wide(r2_), ALU.mult))
                dve.tensor_tensor(WDN[:, s % 2], O1, O2, ALU.add).then_inc(wdn_ready, 1)

            def add_b2(s):
                dve.wait_ge(b_filled, b_uses["b2", s] + 1)
                dve.tensor_tensor(X2[:, s % 2], X2[:, s % 2],
                                  PS[:, Bk, 0:TILES * C].rearrange("p (t c) -> p t c", t=TILES),
                                  ALU.add).then_inc(b_read, 1)

            def combine(s, eh):
                dve.wait_ge(wdn_ready, s + 1)
                dve.wait_ge(w2_done, E * s + 4 * eh + 4)
                for tp in range(2):
                    i = dve.tensor_tensor(
                        PROD[:, :, :].rearrange("p (t e) c -> p t e c", t=2),
                        PS[:, Y_BANK0 + 2 * eh + tp, :].rearrange("p (t e c) -> p t e c", t=2, c=C),
                        WDN[:, s % 2, 2 * tp:2 * tp + 2, 4 * eh:4 * eh + 4].unsqueeze(3).broadcast_to([128, 2, 4, C]),
                        ALU.mult)
                    i.then_inc(y_read, 1)
                    dve.wait_ge(y_read, 2 * (2 * s + eh) + tp + 1)
                    link(dve.tensor_reduce(RED[:, eh, 2 * tp:2 * tp + 2, :],
                                           PROD[:, :, :].rearrange("p (t e) c -> p t c e", t=2), AX.X, ALU.add))

            def finish(s):
                link(dve.tensor_tensor(RED[:, 0], RED[:, 0], RED[:, 1], ALU.add))
                dve.wait_ge(b_read, b_uses["b2", s] + 1)
                if s >= 2:
                    dve.wait_ge(a_filled, a_uses["fin", s - 2] + 1)
                dve.tensor_tensor(FIN[:, s % 2], X2[:, s % 2], RED[:, 0], ALU.add).then_inc(fin_ready, 1)

            dve.wait_ge(conv_moved, 8)
            dve.wait_ge(cst_in, 16)
            mask_k(0)
            mask_k(1)
            read_kv(0)
            attend(0)
            dve.wait_ge(xb_ready, 2)
            norm(0)
            scale(0)
            low_xs(0)
            for s in range(PAIRS):
                top2(s)
                if s + 1 < PAIRS:
                    read_kv(s + 1)
                    attend(s + 1)
                    if s + 2 < PAIRS:
                        mask_k(s + 2)
                combine(s, 0)
                add_b2(s)
                if s + 1 < PAIRS:
                    norm(s + 1)
                    scale(s + 1)
                    low_xs(s + 1)
                combine(s, 1)
                finish(s)

        @block.tensor
        def _(pe):
            def mm(bank, cols, lhsT, rhs, start, stop, parts=128):
                return pe.matmul(PS[0:parts, bank, cols[0]:cols[1]], lhsT, rhs, start=start, stop=stop)

            pe.wait_ge(sel_in, 32)
            for k in range(4):
                for j in range(4):
                    xo = 4 * k + j
                    i = mm(RS_BANK0 + k, (120 * j, 120 * j + 120), SEL[:, (W - 1 - xo) * I:(W - 1 - xo) * I + 128],
                           WD[:, :], True, True)
                i.then_inc(rs_ready, 1)
            pe.wait_ge(x_in, 32)
            pe.wait_ge(cst_in, 16)
            for k in range(2):
                mm(CENTER_BANKS[k], (0, 512), CEN, X[:, 512 * k:512 * k + 512], True, True).then_inc(centred, 1)
            pe.wait_ge(sq_ready, 2)
            for j in range(8):
                i = mm(VAR_BANK, (2 * j, 2 * j + 2), SQ[:, 128 * j:128 * j + 128], ONES, True, True)
            i.then_inc(var_ready, 1)
            pe.wait_ge(xc_ready, 2)
            pe.wait_ge(wq_in, 32)
            for j in range(8):
                if j >= 4:
                    pe.wait_ge(qkv_scaled, j - 3)
                elif QKV_RING[j] == VAR_BANK:
                    pe.wait_ge(var_guarded, 1)
                mm(QKV_RING[j % 4], (0, 2 * QKV), XC[:, 128 * j:128 * j + 128], WQ[:, :], True, True).then_inc(qkv_ready, 1)
            pe.wait_ge(rs_copied, 4)
            for t in range(8):
                i = pe.transpose(PS[:, XT_BANKS[t // 4], 128 * (t % 4):128 * (t % 4) + 128],
                                 X[:, 128 * t:128 * t + 128], IDT)
                if t % 4 == 3:
                    i.then_inc(xt_ready, 1)
            for h in range(8):
                pe.wait_ge(qp_ready, h + 1)
                pe.wait_ge(band_v, 2 * h + 2)
                pe.wait_ge(band_p, h + 1)
                if h == 3:
                    pe.wait_ge(qkv_scaled, 6)
                if h == 2:
                    pe.wait_ge(qkv_scaled, 5)
                if h >= 4:
                    pe.wait_ge(conv_moved, h - 3)
                for q in range(3):
                    for dy in range(DY):
                        i = mm(CONV_RING[h % 4], (128 * q, 128 * q + 128), band[:, 3 * h + q, dy, :],
                               QP[:, 3 * h + q, dy * B:dy * B + 128], dy == 0, dy == DY - 1)
                i.then_inc(conv_ready, 1)

            def a_free(step, s):
                if a_uses[step, s] >= 1:
                    pe.wait_ge(a_read, a_uses[step, s])

            def b_free(step, s):
                if b_uses[step, s] >= 1:
                    pe.wait_ge(b_read, b_uses[step, s])

            def kv(s):
                a_free("kv", s)
                pe.wait_ge(km_ready, 2 * s + 2)
                for b in range(2):
                    for r in range(4):
                        i = mm(A, (KW * b, KW * b + KW), KM[:, s % 2, b, r, :], MS[:, 4 * s + r, 2 * HD:MSW],
                               r == 0, r == 3)
                i.then_inc(a_filled, 1)

            def qt(s):
                b_free("qt", s)
                for r in range(4):
                    i = pe.transpose(PS[:, Bk, 128 * r:128 * r + 128], MS[:, 4 * s + r, 0:HD], IDT)
                i.then_inc(b_filled, 1)

            def num(s):
                a_free("num", s)
                b_free("num", s)
                pe.wait_ge(a_read, a_uses["kv", s] + 1)
                pe.wait_ge(b_read, b_uses["qt", s] + 1)
                for t in range(TILES):
                    i = mm(A + t // 2, (NW * (t % 2), NW * (t % 2) + NW),
                           QT[:, s % 2, t // 2, 128 * (t % 2):128 * (t % 2) + 128], KV[:, s % 2, t // 2, :], True, True)
                    if t == 1:
                        i.then_inc(a_filled, 1)
                i.then_inc(b_filled, 1)

            def attt(s):
                a_free("attt", s)
                pe.wait_ge(a_read, a_uses["num", s] + 1)
                pe.wait_ge(b_read, b_uses["num", s] + 1)
                for t in range(TILES):
                    i = pe.transpose(PS[:, A, 128 * t:128 * t + 128], ATT[:, t, :], IDT)
                i.then_inc(a_filled, 1)

            def proj(s):
                b_free("proj", s)
                pe.wait_ge(a_read, a_uses["attt", s] + 1)
                for t in range(TILES):
                    i = mm(Bk, (C * t, C * t + C), ATTT[:, 128 * t:128 * t + 128], WPS[:, :], True, True)
                i.then_inc(b_filled, 1)

            def xt(s):
                a_free("xt", s)
                pe.wait_ge(xh_ready, s + 1)
                for t in range(TILES):
                    i = pe.transpose(PS[:, A, 128 * t:128 * t + 128], XH2[:, t].rearrange("p k c -> p (k c)"), IDT)
                i.then_inc(a_filled, 1)

            def gate(s):
                b_free("gate", s)
                for t in range(TILES):
                    for k, w in enumerate((WGH, WGL)):
                        i = mm(Bk, (E * t, E * t + E), XS[:, s % 2, 128 * t:128 * t + 128], w[:, :], k == 0, k == 1)
                i.then_inc(b_filled, 1)

            def wdt(s):
                b_free("wdt", s)
                pe.wait_ge(wdn_ready, s + 1)
                pe.transpose(PS[0:TILES * E, Bk, 0:128], WDN[:, s % 2].rearrange("p t e -> p (t e)"), IDT)\
                    .then_inc(b_filled, 1)

            def bias2(s):
                b_free("b2", s)
                pe.wait_ge(b_read, b_uses["wdt", s] + 1)
                mm(Bk, (0, TILES * C), WDT[:, :], B2[:, :], True, True).then_inc(b_filled, 1)

            def fin(s):
                a_free("fin", s)
                pe.wait_ge(fin_ready, s + 1)
                for t in range(TILES):
                    i = pe.transpose(PS[0:C, A, 128 * t:128 * t + 128], FIN[:, s % 2, t, :], IDT)
                i.then_inc(a_filled, 1)

            def first_layer(s, e):
                for k in range(KC * e, KC * e + KC):
                    n = KC * E * s + k
                    if n >= 2:
                        pe.wait_ge(gelu_done, n - 1)
                    for m, w in enumerate((W1H, W1L)):
                        i = mm(H_RING[n % 2], (0, PT), w[:, 128 * k:128 * k + 128], XS[:, s % 2, :], m == 0, m == 1)
                    i.then_inc(h_ready, 1)

            def second_layer(s, e):
                pe.wait_ge(gelu_done, KC * (E * s + e) + KC)
                if s >= 1 and e % 4 == 0:
                    pe.wait_ge(y_read, 2 * (2 * (s - 1) + e // 4) + 2)
                for t in range(TILES):
                    bank = Y_BANK0 + 2 * (e // 4) + t // 2
                    col = C * (4 * (t % 2) + e % 4)
                    for k in range(KC):
                        i = mm(bank, (col, col + C), hidden[:, (KC * (E * s + e) + k) % HRING, 128 * t:128 * t + 128],
                               W2[:, KC * e + k, :], k == 0, k == KC - 1)
                i.then_inc(w2_done, 1)

            pe.wait_ge(conv_moved, 8)
            kv(0)
            qt(0)
            num(0)
            attt(0)
            pe.wait_ge(wps_ready, 1)
            proj(0)
            xt(0)
            pe.wait_ge(w_low, 2)
            pe.wait_ge(w2_in, 16 * 6)
            last = None
            for s in range(PAIRS):
                more = s + 1 < PAIRS
                pe.wait_ge(a_read, a_uses["xt", s] + 1)
                for e in range(E):
                    first_layer(s, e)
                    if last is not None:
                        second_layer(*last)
                    last = (s, e)
                    if e == 0:
                        gate(s)
                        if more:
                            kv(s + 1)
                    if e == 1 and more:
                        qt(s + 1)
                    if e == 2 and more:
                        num(s + 1)
                    if e == 3:
                        wdt(s)
                        if s >= 1:
                            fin(s - 1)
                    if e == 4:
                        bias2(s)
                        if more:
                            attt(s + 1)
                    if e == 5 and more:
                        proj(s + 1)
                    if e == 7 and more:
                        xt(s + 1)
            second_layer(*last)
            fin(PAIRS - 1)


def kernel(x, L0_conv_w_qkv, L0_conv_w_dw, L0_conv_w_pw, L0_conv_w_proj, L0_conv_bn_gamma, L0_conv_bn_beta,
           L0_conv_bn_mean, L0_conv_bn_var, L0_ffn_Wg, L0_ffn_bg, L0_ffn_W1, L0_ffn_b1, L0_ffn_W2, L0_ffn_b2):
    import concourse.bacc as bacc
    from concourse.bass_utils import run_bass_kernel_spmd

    def a(v):
        return np.asarray(v)

    consts, select = constants()
    arrays = {
        "x": a(x),
        "w_qkv": a(L0_conv_w_qkv).T,
        "w_dw": a(L0_conv_w_dw).reshape(G, I, DY, DX).transpose(3, 1, 0, 2).reshape(DX * I, G * DY),
        "w_pw": a(L0_conv_w_pw).transpose(2, 0, 1).reshape(I, G * I),
        "w_proj": a(L0_conv_w_proj).T,
        "vectors": np.concatenate([a(L0_conv_bn_gamma), a(L0_conv_bn_beta), a(L0_conv_bn_mean), a(L0_conv_bn_var),
                                   a(L0_ffn_bg)]),
        "wg": a(L0_ffn_Wg),
        "w1": a(L0_ffn_W1),
        "b1": a(L0_ffn_b1).reshape(E * KC, 128).T,
        "w2": a(L0_ffn_W2).reshape(E * KC, 128, C).transpose(1, 0, 2).reshape(128, E * KC * C),
        "b2": a(L0_ffn_b2),
        "consts": consts,
        "select": select,
    }
    arrays = {f"in_{k}_dram": np.ascontiguousarray(v) for k, v in arrays.items()}
    nc = bacc.Bacc("TRN2", target_bir_lowering=False, num_devices=1)
    args = [nc.dram_tensor(k, v.shape, mybir.dt.from_np(v.dtype), kind="ExternalInput").ap() for k, v in arrays.items()]
    args.append(nc.dram_tensor("out_0_dram", (B, C, H, W), F32, kind="ExternalOutput").ap())
    build(nc, *args)
    r = run_bass_kernel_spmd(nc, [arrays], core_ids=[0])
    return r.results[0]["out_0_dram"]
```

```python
from contextlib import ExitStack

import concourse.bass as bass
from concourse import mybir
import numpy as np

F32 = mybir.dt.float32
F32R = mybir.dt.float32r
ALU = mybir.AluOpType
ACT = mybir.ActivationFunctionType
AX = mybir.AxisListType

B, C, H, W = 8, 64, 16, 16
N = H * W
G, I = 24, 8
QKV = G * I
DY = DX = 5
PAD = DY // 2
YP = H + 2 * PAD
HEADS = 16
HD = HEADS * I
MSW = 3 * HD + 1
KW = HD + 1
NW = HD + HEADS
E, HID, KC = 8, 256, 2
PAIRS = B // 2
TILES = 4
PT = TILES * 128
GM = 32
GZ = GM * (PAIRS - 1)
GW = 2 * GZ + GM
LN_C_EPS, LN_T_EPS, BN_EPS, ATT_EPS = 1e-6, 1e-5, 1e-5, 1e-15

C_CENTER, C_ONES = 0, 128
C_IDENT = C_ONES + 2
C_HEAD = C_IDENT + 128
C_PAR = C_HEAD + HEADS
C_REV = C_PAR + 2
C_END = C_REV + E
SELW = (2 * W - 1) * I
LOW = 64


def constants():
    c = np.zeros((128, C_END), np.float32)
    p = np.arange(128)
    half = p // C
    same = half[:, None] == half[None, :]
    c[:, C_CENTER:C_CENTER + 128] = np.eye(128) - same / C
    c[:, C_ONES:C_ONES + 2] = (half[:, None] == np.arange(2)) / C
    c[:, C_IDENT:C_IDENT + 128] = np.eye(128)
    c[:, C_HEAD:C_HEAD + HEADS] = (p // I)[:, None] == np.arange(HEADS)
    c[:, C_PAR:C_PAR + 2] = ((p // H) % 2)[:, None] == np.arange(2)
    c[:, C_REV:C_REV + E] = E - np.arange(E)
    s = np.zeros((DX, I, 2 * W - 1, I), np.float32)
    for dx in range(DX):
        for i in range(I):
            s[dx, i, dx - PAD + W - 1, i] = 1
    both = np.zeros((LOW + DX * I, SELW), np.float32)
    both[0:DX * I] = both[LOW:] = s.reshape(DX * I, SELW)
    return c, both


def build(nc, x, w_qkv, w_dw, w_pw, w_proj, vectors, wg, w1, b1, w2, b2, consts, select, out):
    ctx = ExitStack()
    with ctx:
        def sb(name, shape, dt=F32):
            return ctx.enter_context(nc.sbuf_tensor(name, shape, dt))

        def sem(name):
            return ctx.enter_context(nc.semaphore(name))

        X = sb("X", [128, 4 * N])
        CST = sb("CST", [128, C_END])
        SELF = sb("SELF", [LOW + DX * I, SELW])
        WDF = sb("WDF", [LOW + DX * I, G * DY])
        PW = sb("PW", [128, G, I])
        WQ = sb("WQ", [128, 2 * QKV])
        WP = sb("WP", [128, C])
        VEC = sb("VEC", [128, 4 * C + E])
        WG = sb("WG", [128, GW])
        W1 = sb("W1", [128, E * HID])
        B1 = sb("B1", [128, E * KC])
        W2 = sb("W2", [128, E * KC, C])
        B2 = sb("B2", [128, E])
        INV = sb("INV", [128, 2, C])
        BIAS = sb("BIAS", [128, C])
        HALF = sb("HALF", [128, TILES])
        EULER = sb("EULER", [128, 16])
        EPS1 = sb("EPS1", [128, 1])
        WPS = sb("WPS", [128, 2, C])
        WPM = sb("WPM", [128, 1])
        SEL = sb("SEL", [LOW + DX * I, SELW], F32R)
        WD = sb("WD", [LOW + DX * I, G * DY], F32R)
        WGH, WGL = sb("WGH", [128, GW], F32R), sb("WGL", [128, GW], F32R)
        W1H, W1L = sb("W1H", [128, E * HID], F32R), sb("W1L", [128, E * HID], F32R)
        RS = sb("RS", [128, G, DY, W])
        BAND = sb("BAND", [128, G * DY * 128])
        XC = sb("XC", [128, 4 * N])
        SQ = sb("SQ", [128, 4 * N])
        DEV1 = sb("DEV1", [128, 16])
        R1 = sb("R1", [128, 8, 2])
        MS = sb("MS", [128, 16, MSW])
        QP = sb("QP", [128, G, YP * B])
        XB = sb("XB", [128, 2, 16, C])
        XBM = sb("XBM", [128, 16])
        GATES = sb("GATES", [128, PT])
        SQ2 = sb("SQ2", [128, 2, TILES, C + 1])
        outs = sb("outs", [128, PAIRS, N])
        WY = sb("WY", [128, 2, N])
        KM = sb("KM", [128, PAIRS, 2, 4, HD])
        DEN = sb("DEN", [128, 2, TILES, HEADS])
        SM = sb("SM", [128, PAIRS, 2, TILES])
        XS = sb("XS", [128, PAIRS, PT], F32R)
        TS = sb("TS", [128, 8, 16])
        WDN = sb("WDN", [128, PAIRS, 2, 2, E])

        band = BAND[:, :].rearrange("p (g d m) -> p g d m", g=G, d=DY)

        taken = [0]

        def late(*dims):
            first = taken[0]
            taken[0] += int(np.prod(dims))
            assert taken[0] <= G * DY * 128
            names = " ".join("abcde"[:len(dims)])
            return BAND[:, first:taken[0]].rearrange(f"p ({names}) -> p {names}", **dict(zip("abcde", dims)))

        HRING = 4
        hidden = late(HRING, PT)
        KV = late(2, 2, NW)
        QT = late(2, 2, N)
        ATT = late(2, TILES, HD)
        ATTT = late(2, PT)
        X2 = late(8, 2, C)
        XC2 = late(2, TILES, C)
        XH2 = late(2, TILES, 2, C)

        TOP = late(6, 16, E)
        WB = late(2, E, N)
        WIDE = late(E // 2, 2, 2, 2, C)

        CEN = CST[:, C_CENTER:C_CENTER + 128]
        ONES = CST[:, C_ONES:C_ONES + 2]
        IDT = CST[:, C_IDENT:C_IDENT + 128]
        PAR = CST[:, C_PAR:C_PAR + 2]

        PS = ctx.enter_context(nc.psum_tensor("PS", [128, 8, 512], F32))
        CENTER_BANKS, VAR_BANK = (0, 1), 2
        RS_BANK0 = 3
        QKV_RING = (7, 0, 1, 2)
        XT_BANKS = (3, 4)
        CONV_RING = (5, 6, 7, 0)
        CHAIN_BANK = (6, 0, 2, 4)
        Y_BANK0 = 0
        H_RING = (6, 7)
        MISC = (4, 5)
        MISC_USES = 1 + E // 2
        MISC_SLOT = (7, 7, 7, 8, 9, 10, 10, 11, 12, 13, 14, 15, 17, 18, 20, 21, 23, 25, 26, 28)

        x_in, cst_in, sel_in, pw_in, wq_in = sem("x_in"), sem("cst_in"), sem("sel_in"), sem("pw_in"), sem("wq_in")
        vec_in, w1_in, w2_in = sem("vec_in"), sem("w1_in"), sem("w2_in")
        b1_in, b2_in = sem("b1_in"), sem("b2_in")
        wq_zero, wd_zero, wg_zero = sem("wq_zero"), sem("wd_zero"), sem("wg_zero")
        pads_set = sem("pads_set")
        sel_high, wd_split = sem("sel_high"), sem("wd_split")
        rs_ready, rs_copied = sem("rs_ready"), sem("rs_copied")
        centred, xc_ready, sq_ready = sem("centred"), sem("xc_ready"), sem("sq_ready")
        var_ready, dev1_ready, r1_ready = sem("var_ready"), sem("dev1_ready"), sem("r1_ready")
        qkv_ready, scaled_v, scaled_s = sem("qkv_ready"), sem("scaled_v"), sem("scaled_s")
        qp_ready = sem("qp_ready")
        band_v, band_p = sem("band_v"), sem("band_p")
        conv_ready, conv_moved = sem("conv_ready"), sem("conv_moved")
        xt_ready, xb_ready = sem("xt_ready"), sem("xb_ready")
        bn_guarded, inv_ready, wps_ready = sem("bn_guarded"), sem("inv_ready"), sem("wps_ready")
        w_high, w_low = sem("w_high"), sem("w_low")
        km_ready, sq2_wanted, sq2_ready = sem("km_ready"), sem("sq2_wanted"), sem("sq2_ready")
        v2_ready, r2_ready, xh_ready, hi_ready = sem("v2_ready"), sem("r2_ready"), sem("xh_ready"), sem("hi_ready")
        a_filled, a_read = ([sem(f"a_{k}{s}") for s in range(PAIRS)] for k in ("filled", "read"))
        b_filled, b_read = ([sem(f"b_{k}{s}") for s in range(PAIRS)] for k in ("filled", "read"))
        A_KV, A_NUM, A_ATTT, A_XT = 1, 2, 3, 4
        B_QT, B_NUM, B_PROJ = 1, 2, 3
        gate_ready, gate_read, gates_turned, gates_copied, gap_ready, exp_ready = sem("gate_ready"), sem("gate_read"), sem("gates_turned"), sem("gates_copied"), sem("gap_ready"), sem("exp_ready")
        wdn_ready, wide_ready = sem("wdn_ready"), sem("wide_ready")
        misc_ready, misc_read = sem("misc_ready"), sem("misc_read")
        h_ready, gelu_done, w2_done, y_read = sem("h_ready"), sem("gelu_done"), sem("w2_done"), sem("y_read")
        out_ready, stored = sem("out_ready"), sem("stored")
        v_chain, p_chain = sem("v_chain"), sem("p_chain")

        def by_pixel(k):
            return PS[:, CENTER_BANKS[k], :].rearrange("p (t q r) -> p r q t", q=4, r=4)

        def pair_tokens(t, k):
            return t[:, 512 * k:512 * k + 512].rearrange("p (r q t) -> p r q t", q=4, r=4)

        def qkv_heads(j, h):
            pair, xr = divmod(j, 4)
            return (MS[:, 4 * (2 * h + pair) + xr, 0:3 * HD].rearrange("p (q h i) -> p h q i", q=3, i=I)[:, 0:8],
                    PS[:, QKV_RING[j % 4], QKV * h:QKV * h + QKV].rearrange("p (h q i) -> p h q i", q=3, i=I))

        def head(h):
            return MS[:, :, 0:3 * HD].rearrange("p j (q h i) -> p h q j i", q=3, i=I)[:, h]

        def band_factors(g):
            return (band[:, g].rearrange("p d (x o) -> p (d x) o", o=I),
                    RS[:, g].rearrange("p d x -> p (d x)").unsqueeze(2).broadcast_to([128, DY * W, I]),
                    PW[:, g, :].unsqueeze(1).broadcast_to([128, DY * W, I]))

        block = ctx.enter_context(nc.Block())

        @block.sync
        def _(sp):
            xs = x.rearrange("(h b) c y x -> h c b (y x)", h=2)
            for h in range(2):
                sp.dma_start(X[C * h:C * h + C, :].rearrange("c (b n) -> c b n", b=4), xs[h]).then_inc(x_in, 16)
            sp.wait_ge(wq_zero, 1)
            for h in range(2):
                sp.dma_start(WQ[C * h:C * h + C, QKV * h:QKV * h + QKV], w_qkv).then_inc(wq_in, 16)
            sp.dma_start(VEC[:, :], vectors.unsqueeze(0).broadcast_to([128, 4 * C + E])).then_inc(vec_in, 16)
            sp.dma_start(WP[:, :], w_proj).then_inc(vec_in, 16)
            sp.wait_ge(wg_zero, 1)
            for h in range(2):
                sp.dma_start(WG[C * h:C * h + C, GZ:GZ + E], wg).then_inc(w1_in, 16)
                sp.dma_start(W1[C * h:C * h + C, :].rearrange("c (e n) -> c e n", e=E),
                             w1.rearrange("e c n -> c e n")).then_inc(w1_in, 16)
            for h in range(2):
                sp.dma_start(B2[C * h:C * h + C, :], b2).then_inc(b2_in, 16)
            for s in range(PAIRS):
                sp.wait_ge(out_ready, s + 1)
                sp.dma_start(out[2 * s:2 * s + 2].rearrange("b c y x -> (b c) (y x)"), outs[:, s, :]).then_inc(stored, 16)
            sp.wait_ge(stored, 16 * PAIRS)

        @block.gpsimd
        def _(pool):
            pool.memset(WDF[:, :], 0.0).then_inc(wd_zero, 1)
            pool.memset(WQ[:, :], 0.0).then_inc(wq_zero, 1)
            pool.memset(WG[:, :], 0.0).then_inc(wg_zero, 1)
            pool.memset(EPS1[:, :], LN_C_EPS).then_inc(pads_set, 1)
            pool.memset(HALF[:, :], -0.5).then_inc(pads_set, 1)
            pool.memset(EULER[:, :], float(np.e)).then_inc(pads_set, 1)
            pool.memset(QP[:, :, 0:PAD * B], 0.0).then_inc(pads_set, 1)
            pool.memset(QP[:, :, (PAD + H) * B:YP * B], 0.0).then_inc(pads_set, 1)
            pool.memset(SQ2[:, :, :, C:C + 1], LN_T_EPS).then_inc(pads_set, 1)
            pool.memset(MS[:, :, 3 * HD:MSW], 1.0).then_inc(pads_set, 1)
            pool.wait_ge(pads_set, 7)
            pool.wait_ge(rs_copied, 4)
            pool.wait_ge(pw_in, 16)
            for g in range(2, G, 3):
                pool.tensor_tensor(*band_factors(g), ALU.mult).then_inc(band_p, 1)
            pool.wait_ge(w_high, 2)
            pool.tensor_tensor(W1L[:, :], W1[:, :], W1H[:, :].bitcast(F32), ALU.subtract).then_inc(w_low, 1)
            pool.tensor_tensor(WGL[:, :], WG[:, :], WGH[:, :].bitcast(F32), ALU.subtract).then_inc(w_low, 1)
            for s in range(PAIRS):
                pool.wait_ge(v2_ready, s + 1)
                pool.tensor_tensor(SM[:, s, 1, :], SM[:, s, 0, :], HALF[:, :], ALU.pow).then_inc(r2_ready, 1)
            pool.wait_ge(gap_ready, 1)
            pool.tensor_tensor(TS[:, 5, :], EULER[:, :], TS[:, 4, :], ALU.pow).then_inc(exp_ready, 1)
            pool.wait_ge(wdn_ready, 2)
            for s in range(PAIRS):
                for ep in range(E // 2):
                    if s >= 1:
                        pool.wait_ge(misc_ready, MISC_USES * (s - 1) + 2 + ep)
                    pool.tensor_copy(
                        WIDE[:, ep].rearrange("p e h b c -> p e (h b) c"),
                        WDN[:, s, :, :, 2 * ep:2 * ep + 2].rearrange("p h b e -> p e (h b)").unsqueeze(3)
                        .broadcast_to([128, 2, 4, C])).then_inc(wide_ready, 1)

        @block.scalar
        def _(act):
            act.wait_ge(wd_zero, 1)
            act.dma_start(WDF[0:DX * I, :], w_dw).then_inc(sel_in, 16)
            act.dma_start(WDF[LOW:LOW + DX * I, :], w_dw).then_inc(sel_in, 16)
            act.dma_start(CST[:, :], consts).then_inc(cst_in, 16)
            act.dma_start(SELF[:, :], select).then_inc(sel_in, 16)
            act.dma_start(PW[:, :, :].rearrange("p g o -> p (g o)"),
                          w_pw.unsqueeze(0).broadcast_to([W, I, QKV])).then_inc(pw_in, 16)
            act.dma_start(W2[:, :, :].rearrange("p k c -> p (k c)"), w2).then_inc(w2_in, 16)
            act.dma_start(B1[:, :], b1).then_inc(b1_in, 16)
            act.wait_ge(sel_in, 48)
            act.activation(SEL[:, :], SELF[:, :], ACT.Copy).then_inc(sel_high, 1)
            for k in range(2):
                act.wait_ge(centred, k + 1)
                act.activation(pair_tokens(SQ, k), by_pixel(k), ACT.Square).then_inc(sq_ready, 1)
            for k in range(4):
                act.wait_ge(rs_ready, k + 1)
                act.activation(RS[:, :, :, 4 * k:4 * k + 4].rearrange("p g d x -> p (g d) x"),
                               PS[:, RS_BANK0 + k, 0:480].rearrange("p (x m) -> p m x", x=4),
                               ACT.Copy).then_inc(rs_copied, 1)
            act.wait_ge(var_ready, 1)
            act.wait_ge(pads_set, 7)
            act.activation(DEV1[:, :], PS[:, VAR_BANK, 0:16], ACT.Sqrt, bias=EPS1[:, :]).then_inc(dev1_ready, 1)
            act.wait_ge(r1_ready, 1)
            for j in range(1, 8, 2):
                act.wait_ge(qkv_ready, j + 1)
                for h in range(2):
                    to, of = qkv_heads(j, h)
                    i = act.activation(to, of, ACT.Copy, scale=R1[:, j, h:h + 1])
                i.then_inc(scaled_s, 1)
            act.wait_ge(bn_guarded, 1)
            act.activation(INV[:, 1, :], INV[:, 0, :], ACT.Sqrt).then_inc(inv_ready, 1)
            act.wait_ge(w1_in, 64)
            act.activation(W1H[:, :], W1[:, :], ACT.Copy).then_inc(w_high, 1)
            act.activation(WGH[:, :], WG[:, :], ACT.Copy).then_inc(w_high, 1)

            def relu_qt(s):
                act.wait_ge(b_filled[s], B_QT)
                if s >= 2:
                    act.wait_ge(b_filled[s - 2], B_NUM)
                for b in range(2):
                    i = act.activation(
                        QT[:, s % 2, b, :].rearrange("p (y q r) -> p r q y", q=4, r=4),
                        PS[:, CHAIN_BANK[s] + 1, :].rearrange("p (r q b y) -> p b r q y", r=4, q=4, b=2)[:, b],
                        ACT.Relu)
                i.then_inc(b_read[s], 1)

            def copy_attt(s):
                act.wait_ge(a_filled[s], A_ATTT)
                if s >= 2:
                    act.wait_ge(b_filled[s - 2], B_PROJ)
                act.activation(ATTT[:, s % 2, :], PS[:, CHAIN_BANK[s], :], ACT.Copy).then_inc(a_read[s], 1)

            def square_xc(s):
                act.wait_ge(sq2_wanted, s + 1)
                if s >= 2:
                    act.wait_ge(v2_ready, s - 1)
                act.activation(SQ2[:, s % 2, :, 0:C], XC2[:, s % 2], ACT.Square, scale=C ** -0.5).then_inc(sq2_ready, 1)

            def high_xs(s):
                act.wait_ge(a_filled[s], A_XT)
                act.activation(XS[:, s, :], PS[:, CHAIN_BANK[s], :], ACT.Copy).then_inc(hi_ready, 1)

            def gelu(s, e):
                for k in range(KC * e, KC * e + KC):
                    n = KC * E * s + k
                    act.wait_ge(h_ready, n + 1)
                    if n >= HRING:
                        act.wait_ge(w2_done, n // KC - 1)
                    act.activation(hidden[:, n % HRING, :], PS[:, H_RING[n % 2], :], ACT.Gelu,
                                   bias=B1[:, k:k + 1]).then_inc(gelu_done, 1)

            act.wait_ge(b1_in, 16)
            relu_qt(0)
            relu_qt(1)
            relu_qt(2)
            copy_attt(0)
            square_xc(0)
            relu_qt(3)
            copy_attt(1)
            square_xc(1)
            high_xs(0)
            copy_attt(2)
            square_xc(2)
            gelu(0, 0)
            copy_attt(3)
            high_xs(1)
            square_xc(3)
            gelu(0, 1)
            high_xs(2)
            gelu(0, 2)
            high_xs(3)
            for s in range(PAIRS):
                for e in range(3 if s == 0 else 0, E):
                    gelu(s, e)

        @block.vector
        def _(dve):
            chain = [0]

            def link(i):
                chain[0] += 1
                i.then_inc(v_chain, 1)
                dve.wait_ge(v_chain, chain[0])

            def bands(g):
                dve.tensor_tensor(*band_factors(g), ALU.mult).then_inc(band_v, 1)

            dve.wait_ge(sel_in, 48)
            link(dve.tensor_copy(WD[:, :], WDF[:, :]))
            dve.tensor_tensor(WD[LOW:LOW + DX * I, :], WDF[LOW:LOW + DX * I, :], WD[LOW:LOW + DX * I, :].bitcast(F32),
                              ALU.subtract).then_inc(wd_split, 1)
            for k in range(2):
                dve.wait_ge(centred, k + 1)
                dve.wait_ge(sq_ready, k + 1)
                dve.tensor_copy(pair_tokens(XC, k), by_pixel(k)).then_inc(xc_ready, 1)
            dve.wait_ge(rs_copied, 4)
            dve.wait_ge(pw_in, 16)
            bands(0)
            dve.wait_ge(dev1_ready, 1)
            dve.reciprocal(R1[:, :, :].rearrange("p j h -> p (j h)"), DEV1[:, :]).then_inc(r1_ready, 1)
            dve.wait_ge(r1_ready, 1)
            for j in range(0, 8, 2):
                dve.wait_ge(qkv_ready, j + 1)
                for h in range(2):
                    to, of = qkv_heads(j, h)
                    i = dve.tensor_scalar(to, of, R1[:, j, h:h + 1], None, ALU.mult)
                i.then_inc(scaled_v, 1)
            bands(1)
            dve.wait_ge(scaled_v, 4)
            dve.wait_ge(scaled_s, 4)
            dve.wait_ge(pads_set, 7)
            qp = QP[:, :, :].rearrange("p g (y b) -> p g b y", b=B)

            def move_head(h):
                dve.wait_ge(conv_ready, h + 1)
                dve.transpose(head(8 + h), PS[:, CONV_RING[h % 4], 0:3 * 128].rearrange("p (q y b) -> p q b y", q=3, b=B))\
                    .then_inc(conv_moved, 1)

            def mask_k(s, half):
                for b in range(2):
                    dve.tensor_scalar(KM[:, s, b, :, C * half:C * half + C],
                                      MS[:, 4 * s:4 * s + 4, HD + C * half:HD + C * half + C],
                                      0.0, PAR[:, b:b + 1], ALU.max, ALU.mult).then_inc(km_ready, 1)

            for h in range(8):
                dve.transpose(qp[:, 3 * h:3 * h + 3, :, PAD:PAD + H], head(h)).then_inc(qp_ready, 1)
                if h >= 1:
                    bands(3 * h)
                    bands(3 * h + 1)
                if h >= 3:
                    move_head(h - 3)
                if h == 1:
                    dve.wait_ge(vec_in, 32)
                    dve.tensor_scalar(INV[:, 0, :], VEC[:, 3 * C:4 * C], BN_EPS, None, ALU.add).then_inc(bn_guarded, 1)
                if h == 4:
                    dve.wait_ge(inv_ready, 1)
                    link(dve.reciprocal(INV[:, 0, :], INV[:, 1, :]))
                    link(dve.tensor_tensor(INV[:, 0, :], INV[:, 0, :], VEC[:, 0:C], ALU.mult))
                    link(dve.tensor_tensor(BIAS[:, :], VEC[:, 2 * C:3 * C], INV[:, 0, :], ALU.mult))
                    link(dve.tensor_tensor(BIAS[:, :], VEC[:, C:2 * C], BIAS[:, :], ALU.subtract))
                    link(dve.tensor_tensor(WPS[:, 0, :], WP[:, :], INV[:, 0, :], ALU.mult))
                    link(dve.tensor_reduce(WPM[:, :], WPS[:, 0, :], AX.X, ALU.add))
                    dve.scalar_tensor_tensor(out=WPS[:, 1, :], in0=WPM[:, :].broadcast_to([128, C]), scalar=-1.0 / C,
                                             in1=WPS[:, 0, :], op0=ALU.mult, op1=ALU.add).then_inc(wps_ready, 1)
                if h == 5:
                    for k in range(2):
                        dve.wait_ge(xt_ready, k + 1)
                        i = dve.tensor_tensor(
                            XB[:, 0, :, :].rearrange("p (h t) c -> p t h c", h=2)[:, 4 * k:4 * k + 4],
                            PS[:, XT_BANKS[k], :].rearrange("p (t h c) -> p t h c", t=4, h=2),
                            BIAS[:, :].unsqueeze(1).unsqueeze(1).broadcast_to([128, 4, 2, C]), ALU.add)
                        i.then_inc(xb_ready, 1)
                if h == 6:
                    dve.wait_ge(xb_ready, 2)
                    link(dve.tensor_reduce(XBM[:, :], XB[:, 0, :, :], AX.X, ALU.add))
                    link(dve.scalar_tensor_tensor(out=XB[:, 1, :, :], in0=XBM[:, :].unsqueeze(2).broadcast_to([128, 16, C]),
                                                  scalar=-1.0 / C, in1=XB[:, 0, :, :], op0=ALU.mult, op1=ALU.add))
            move_head(5)
            for s in range(PAIRS):
                mask_k(s, 0)
            move_head(6)
            move_head(7)
            dve.wait_ge(conv_moved, 8)

            def read_kv(s):
                dve.wait_ge(a_filled[s], A_KV)
                if s >= 2:
                    dve.wait_ge(b_filled[s - 2], B_NUM)
                kv = PS[:, CHAIN_BANK[s], 0:2 * KW].rearrange("p (b v) -> p b v", b=2)
                own = CST[:, C_HEAD:C_HEAD + HEADS].unsqueeze(1)
                dve.tensor_tensor(KV[:, s % 2, :, 0:HD].rearrange("p b (h v) -> p b h v", v=I),
                                  kv[:, :, 0:HD].rearrange("p b (h v) -> p b h v", v=I),
                                  own.unsqueeze(3).broadcast_to([128, 2, HEADS, I]), ALU.mult)
                dve.tensor_tensor(KV[:, s % 2, :, HD:NW], kv[:, :, HD:KW].broadcast_to([128, 2, HEADS]),
                                  own.broadcast_to([128, 2, HEADS]), ALU.mult).then_inc(a_read[s], 1)

            def attend(s):
                dve.wait_ge(a_filled[s], A_NUM)
                dve.wait_ge(b_filled[s], B_NUM)
                nd = PS[:, CHAIN_BANK[s]:CHAIN_BANK[s] + 2, 0:2 * NW].rearrange("p k (t v) -> p k t v", t=2)
                link(dve.tensor_scalar(DEN[:, 0, :, :].rearrange("p (k t) h -> p k t h", k=2), nd[:, :, :, HD:NW],
                                       ATT_EPS, None, ALU.add))
                link(dve.reciprocal(DEN[:, 1, :, :].rearrange("p t h -> p (t h)"),
                                    DEN[:, 0, :, :].rearrange("p t h -> p (t h)")))
                if s >= 2:
                    dve.wait_ge(a_filled[s - 2], A_ATTT)
                for k, read in enumerate((a_read[s], b_read[s])):
                    dve.tensor_tensor(
                        ATT[:, s % 2, 2 * k:2 * k + 2, :].rearrange("p t (h v) -> p t h v", v=I),
                        nd[:, k, :, 0:HD].rearrange("p t (h v) -> p t h v", v=I),
                        DEN[:, 1, 2 * k:2 * k + 2, :].unsqueeze(3).broadcast_to([128, 2, HEADS, I]), ALU.mult)\
                        .then_inc(read, 1)

            def residual(s):
                dve.wait_ge(b_filled[s], B_PROJ)
                both = PS[:, CHAIN_BANK[s] + 1, :].rearrange("p (t k c) -> p k t c", t=TILES, k=2)
                if s >= 2:
                    dve.wait_ge(xh_ready, s - 1)
                dve.tensor_tensor(XC2[:, s % 2], both[:, 1], XB[:, 1, TILES * s:TILES * s + TILES, :], ALU.add)\
                    .then_inc(sq2_wanted, 1)
                dve.tensor_tensor(X2[:, 2 * s:2 * s + 2].rearrange("p h b c -> p b h c"),
                                  both[:, 0].rearrange("p (b h) c -> p b h c", b=2),
                                  XB[:, 0, TILES * s:TILES * s + TILES, :].rearrange("p (b h) c -> p b h c", b=2),
                                  ALU.add).then_inc(b_read[s], 1)

            def variance(s):
                dve.wait_ge(sq2_ready, s + 1)
                dve.tensor_reduce(SM[:, s, 0, :], SQ2[:, s % 2], AX.X, ALU.add).then_inc(v2_ready, 1)

            def scale(s):
                dve.wait_ge(r2_ready, s + 1)
                dve.wait_ge(sq2_wanted, s + 1)
                if s >= 2:
                    dve.wait_ge(a_filled[s - 2], A_XT)
                dve.tensor_tensor(XH2[:, s % 2], XC2[:, s % 2].unsqueeze(2).broadcast_to([128, TILES, 2, C]),
                                  SM[:, s, 1, :].unsqueeze(2).unsqueeze(3).broadcast_to([128, TILES, 2, C]),
                                  ALU.mult).then_inc(xh_ready, 1)

            def low_xs(s):
                dve.wait_ge(hi_ready, s + 1)
                dve.tensor_tensor(XS[C:2 * C, s, :], PS[C:2 * C, CHAIN_BANK[s], :], XS[C:2 * C, s, :].bitcast(F32),
                                  ALU.subtract).then_inc(a_read[s], 1)

            def copy_gates():
                dve.wait_ge(gate_ready, 1)
                dve.tensor_copy(GATES[:, :], PS[:, MISC[0], :]).then_inc(gates_copied, 1)

            def top2():
                L, E1, C1, O1, L2, O2 = (TOP[:, k] for k in range(6))
                m1, r, m2, q2, gap, ex, dn, q1 = (TS[:, k] for k in range(8))

                def wide(v):
                    return v.unsqueeze(2).broadcast_to([128, 16, E])

                def rows(v):
                    return v.unsqueeze(1).broadcast_to([128, 16, E])

                rev = rows(CST[:, C_REV:C_REV + E])
                dve.wait_ge(gates_turned, 1)
                dve.tensor_tensor(L.rearrange("p (s t) e -> p s t e", t=TILES),
                                  PS[:, MISC[1], :].rearrange("p (t s e) -> p s t e", t=TILES, e=GM)[:, :, :, 0:E],
                                  VEC[:, 4 * C:4 * C + E].unsqueeze(1).unsqueeze(1).broadcast_to([128, PAIRS, TILES, E]),
                                  ALU.add).then_inc(gate_read, 1)
                dve.wait_ge(gate_read, 1)
                for lg, m, o in ((L, m1, O1), (L2, m2, O2)):
                    link(dve.tensor_reduce(m, lg, AX.X, ALU.max))
                    if o is O2:
                        dve.tensor_tensor(gap, m2, m1, ALU.subtract).then_inc(gap_ready, 1)
                    link(dve.tensor_tensor(E1, lg, wide(m), ALU.is_equal))
                    link(dve.tensor_tensor(C1, E1, rev, ALU.mult))
                    link(dve.tensor_reduce(r, C1, AX.X, ALU.max))
                    link(dve.tensor_tensor(o, C1, wide(r), ALU.is_equal))
                    if o is O1:
                        link(dve.scalar_tensor_tensor(out=L2, in0=O1, scalar=-3e38, in1=L, op0=ALU.mult, op1=ALU.add))

            def softmax():
                O1, O2 = TOP[:, 3], TOP[:, 5]
                q2, ex, dn, q1 = (TS[:, k] for k in (3, 5, 6, 7))

                def wide(v):
                    return v.unsqueeze(2).broadcast_to([128, 16, E])

                dve.wait_ge(exp_ready, 1)
                link(dve.tensor_scalar(dn, ex, 1.0, None, ALU.add))
                link(dve.reciprocal(q1, dn))
                link(dve.tensor_tensor(q2, ex, q1, ALU.mult))
                link(dve.tensor_tensor(O1, O1, wide(q1), ALU.mult))
                link(dve.tensor_tensor(O2, O2, wide(q2), ALU.mult))
                for b in range(2):
                    dve.tensor_tensor(WDN[:, :, :, b, :], O1.rearrange("p (s b h) e -> p b s h e", b=2, h=2)[:, b],
                                      O2.rearrange("p (s b h) e -> p b s h e", b=2, h=2)[:, b], ALU.add).then_inc(wdn_ready, 1)

            def read_tokens(s):
                n = MISC_USES * s
                dve.wait_ge(misc_ready, n + 1)
                dve.tensor_copy(outs[:, s, :], PS[:, MISC[n % 2], 0:N]).then_inc(misc_read, 1)

            def read_weights(s, ep):
                n = MISC_USES * s + 1 + ep
                dve.wait_ge(misc_ready, n + 1)
                dve.tensor_copy(WB[:, s % 2, 2 * ep:2 * ep + 2, :].rearrange("p e n -> p (e n)"),
                                PS[:, MISC[n % 2], :]).then_inc(misc_read, 1)

            def combine(s, e):
                dve.wait_ge(w2_done, E * s + 2 * (e // 2) + 2)
                dve.wait_ge(misc_read, MISC_USES * s + 2 + e // 2)
                dve.scalar_tensor_tensor(out=WY[:, e % 2, :], in0=PS[:, Y_BANK0 + e // 2, N * (e % 2):N * (e % 2) + N],
                                         scalar=B2[:, e:e + 1], in1=WB[:, s % 2, e, :], op0=ALU.add, op1=ALU.mult)\
                    .then_inc(y_read, 1)
                dve.wait_ge(y_read, E * s + e + 1)
                i = dve.tensor_tensor(outs[:, s, :], outs[:, s, :], WY[:, e % 2, :], ALU.add)
                if e == E - 1:
                    i.then_inc(out_ready, 1)
                else:
                    link(i)

            mask_k(0, 1)
            mask_k(1, 1)
            read_kv(0)
            mask_k(2, 1)
            read_kv(1)
            attend(0)
            mask_k(3, 1)
            read_kv(2)
            attend(1)
            residual(0)
            variance(0)
            read_kv(3)
            scale(0)
            attend(2)
            residual(1)
            low_xs(0)
            variance(1)
            attend(3)
            scale(1)
            residual(2)
            variance(2)
            low_xs(1)
            scale(2)
            residual(3)
            variance(3)
            low_xs(2)
            scale(3)
            low_xs(3)
            copy_gates()
            top2()
            softmax()
            dve.wait_ge(b2_in, 32)
            read_tokens(0)
            read_weights(0, 0)
            for s in range(PAIRS):
                for e in range(E):
                    combine(s, e)
                    if e % 2 == 0 and e < E - 2:
                        read_weights(s, e // 2 + 1)
                    elif e == E - 2 and s < PAIRS - 1:
                        read_tokens(s + 1)
                        read_weights(s + 1, 0)

        @block.tensor
        def _(pe):
            def mm(bank, cols, lhsT, rhs, start, stop, parts=128):
                return pe.matmul(PS[0:parts, bank, cols[0]:cols[1]], lhsT, rhs, start=start, stop=stop)

            pe.wait_ge(x_in, 32)
            pe.wait_ge(cst_in, 16)
            for k in range(2):
                mm(CENTER_BANKS[k], (0, 512), CEN, X[:, 512 * k:512 * k + 512], True, True).then_inc(centred, 1)
            pe.wait_ge(sel_high, 1)
            pe.wait_ge(wd_split, 1)
            for k in range(4):
                for j in range(4):
                    xo = 4 * k + j
                    i = mm(RS_BANK0 + k, (120 * j, 120 * j + 120), SEL[:, (W - 1 - xo) * I:(W - 1 - xo) * I + 128],
                           WD[:, :], True, True)
                i.then_inc(rs_ready, 1)
            pe.wait_ge(sq_ready, 2)
            for j in range(8):
                i = mm(VAR_BANK, (2 * j, 2 * j + 2), SQ[:, 128 * j:128 * j + 128], ONES, True, True)
            i.then_inc(var_ready, 1)
            pe.wait_ge(xc_ready, 2)
            pe.wait_ge(wq_in, 32)
            for j in range(8):
                if j >= 4:
                    pe.wait_ge(scaled_s if j % 2 else scaled_v, (j - 4) // 2 + 1)
                elif QKV_RING[j] == VAR_BANK:
                    pe.wait_ge(dev1_ready, 1)
                mm(QKV_RING[j % 4], (0, 2 * QKV), XC[:, 128 * j:128 * j + 128], WQ[:, :], True, True).then_inc(qkv_ready, 1)
            pe.wait_ge(rs_copied, 4)
            for t in range(8):
                i = pe.transpose(PS[:, XT_BANKS[t // 4], 128 * (t % 4):128 * (t % 4) + 128],
                                 X[:, 128 * t:128 * t + 128], IDT)
                if t % 4 == 3:
                    i.then_inc(xt_ready, 1)
            pe.wait_ge(scaled_v, 4)
            pe.wait_ge(scaled_s, 4)
            for h in range(8):
                pe.wait_ge(qp_ready, h + 1)
                pe.wait_ge(band_v, 2 * h + 2)
                pe.wait_ge(band_p, h + 1)
                if h >= 4:
                    pe.wait_ge(conv_moved, h - 3)
                for q in range(3):
                    for dy in range(DY):
                        i = mm(CONV_RING[h % 4], (128 * q, 128 * q + 128), band[:, 3 * h + q, dy, :],
                               QP[:, 3 * h + q, dy * B:dy * B + 128], dy == 0, dy == DY - 1)
                i.then_inc(conv_ready, 1)

            def kv(s):
                pe.wait_ge(km_ready, 2 * (PAIRS + s) + 2)
                for b in range(2):
                    for r in range(4):
                        i = mm(CHAIN_BANK[s], (KW * b, KW * b + KW), KM[:, s, b, r, :], MS[:, 4 * s + r, 2 * HD:MSW],
                               r == 0, r == 3)
                i.then_inc(a_filled[s], 1)

            def qt(s):
                for r in range(4):
                    i = pe.transpose(PS[:, CHAIN_BANK[s] + 1, 128 * r:128 * r + 128], MS[:, 4 * s + r, 0:HD], IDT)
                i.then_inc(b_filled[s], 1)

            def num(s):
                pe.wait_ge(a_read[s], A_KV)
                pe.wait_ge(b_read[s], B_QT)
                for t in range(TILES):
                    i = mm(CHAIN_BANK[s] + t // 2, (NW * (t % 2), NW * (t % 2) + NW),
                           QT[:, s % 2, t // 2, 128 * (t % 2):128 * (t % 2) + 128], KV[:, s % 2, t // 2, :], True, True)
                    if t == 1:
                        i.then_inc(a_filled[s], 1)
                i.then_inc(b_filled[s], 1)

            def attt(s):
                pe.wait_ge(a_read[s], A_NUM)
                pe.wait_ge(b_read[s], B_NUM)
                for t in range(TILES):
                    i = pe.transpose(PS[:, CHAIN_BANK[s], 128 * t:128 * t + 128], ATT[:, s % 2, t, :], IDT)
                i.then_inc(a_filled[s], 1)

            def proj(s):
                pe.wait_ge(a_read[s], A_ATTT)
                pe.wait_ge(wps_ready, 1)
                for t in range(TILES):
                    i = mm(CHAIN_BANK[s] + 1, (128 * t, 128 * t + 128), ATTT[:, s % 2, 128 * t:128 * t + 128],
                           WPS[:, :, :].rearrange("p k c -> p (k c)"), True, True)
                i.then_inc(b_filled[s], 1)

            def xt(s):
                pe.wait_ge(xh_ready, s + 1)
                for t in range(TILES):
                    i = pe.transpose(PS[:, CHAIN_BANK[s], 128 * t:128 * t + 128],
                                     XH2[:, s % 2, t].rearrange("p k c -> p (k c)"), IDT)
                i.then_inc(a_filled[s], 1)

            def gate():
                for s in range(PAIRS):
                    pe.wait_ge(a_read[s], A_XT)
                for s in range(PAIRS):
                    for k, w in enumerate((WGH, WGL)):
                        i = pe.matmul(PS[:, MISC[0], :], w[:, GZ - GM * s:GZ - GM * s + 128], XS[:, s, :],
                                      start=s == k == 0, stop=s == PAIRS - 1 and k == 1)
                i.then_inc(gate_ready, 1)

            def turn_gates():
                pe.wait_ge(gates_copied, 1)
                pe.wait_ge(b_read[PAIRS - 1], B_PROJ)
                for t in range(TILES):
                    i = pe.transpose(PS[:, MISC[1], 128 * t:128 * t + 128], GATES[:, 128 * t:128 * t + 128], IDT)
                i.then_inc(gates_turned, 1)

            def tokens(s):
                n = MISC_USES * s
                if n >= 2:
                    pe.wait_ge(misc_read, n - 1)
                else:
                    pe.wait_ge(gate_read, 1)
                for half in range(2):
                    i = pe.transpose(PS[:, MISC[n % 2], 128 * half:128 * half + 128],
                                     X2[:, 2 * s + half].rearrange("p b c -> p (b c)"), IDT)
                i.then_inc(misc_ready, 1)

            def weights(s, ep):
                n = MISC_USES * s + 1 + ep
                if n >= 2:
                    pe.wait_ge(misc_read, n - 1)
                pe.wait_ge(wide_ready, E // 2 * s + ep + 1)
                for e in range(2):
                    for half in range(2):
                        i = pe.transpose(PS[:, MISC[n % 2], N * e + 128 * half:N * e + 128 * half + 128],
                                         WIDE[:, ep, e, half].rearrange("p b c -> p (b c)"), IDT)
                i.then_inc(misc_ready, 1)

            def first_layer(s, e):
                pe.wait_ge(a_read[s], A_XT)
                if s == e == 0:
                    pe.wait_ge(b_read[0], B_PROJ)
                    pe.wait_ge(w_low, 2)
                for k in range(KC * e, KC * e + KC):
                    n = KC * E * s + k
                    if n >= 2:
                        pe.wait_ge(gelu_done, n - 1)
                    for m, w in enumerate((W1H, W1L)):
                        i = mm(H_RING[n % 2], (0, PT), w[:, 128 * k:128 * k + 128], XS[:, s, :], m == 0, m == 1)
                    i.then_inc(h_ready, 1)

            def second_layer(s, e):
                pe.wait_ge(gelu_done, KC * (E * s + e) + KC)
                if s >= 1:
                    pe.wait_ge(y_read, E * (s - 1) + e + (2 if e % 2 == 0 else 1))
                if s == 0 and e % 4 == 0:
                    owner = 1 + e // 4
                    pe.wait_ge(a_read[owner], A_XT)
                    pe.wait_ge(b_read[owner], B_PROJ)
                if s == e == 0:
                    pe.wait_ge(w2_in, 16)
                for k in range(KC):
                    for b in range(2):
                        i = pe.matmul(PS[C * b:C * b + C, Y_BANK0 + e // 2, N * (e % 2):N * (e % 2) + N],
                                      W2[:, KC * e + k, :], hidden[:, (KC * (E * s + e) + k) % HRING, N * b:N * b + N],
                                      start=k == 0, stop=k == KC - 1)
                i.then_inc(w2_done, 1)

            pe.wait_ge(conv_moved, 8)
            pe.wait_ge(xb_ready, 2)
            kv(0)
            qt(0)
            kv(1)
            qt(1)
            num(0)
            kv(2)
            qt(2)
            attt(0)
            num(1)
            proj(0)
            kv(3)
            qt(3)
            attt(1)
            num(2)
            proj(1)
            xt(0)
            num(3)
            attt(2)
            proj(2)
            for s in range(PAIRS):
                for e in range(E):
                    first_layer(s, e)
                    if s == 0 and e == 0:
                        attt(3)
                        proj(3)
                        xt(1)
                    elif e >= 1:
                        second_layer(s, e - 1)
                    else:
                        second_layer(s - 1, E - 1)
                    if s == 0 and e == 1:
                        xt(2)
                    if s == 0 and e == 2:
                        xt(3)
                    if s == 0 and e == 3:
                        gate()
                    if s == 0 and e == 4:
                        turn_gates()
                    for n in range(MISC_USES * PAIRS):
                        if MISC_SLOT[n] == E * s + e:
                            if n % MISC_USES == 0:
                                tokens(n // MISC_USES)
                            else:
                                weights(n // MISC_USES, n % MISC_USES - 1)
            second_layer(PAIRS - 1, E - 1)


def kernel(x, L0_conv_w_qkv, L0_conv_w_dw, L0_conv_w_pw, L0_conv_w_proj, L0_conv_bn_gamma, L0_conv_bn_beta,
           L0_conv_bn_mean, L0_conv_bn_var, L0_ffn_Wg, L0_ffn_bg, L0_ffn_W1, L0_ffn_b1, L0_ffn_W2, L0_ffn_b2):
    import concourse.bacc as bacc
    from concourse.bass_utils import run_bass_kernel_spmd

    def a(v):
        return np.asarray(v)

    consts, select = constants()
    arrays = {
        "x": a(x),
        "w_qkv": a(L0_conv_w_qkv).T,
        "w_dw": a(L0_conv_w_dw).reshape(G, I, DY, DX).transpose(3, 1, 0, 2).reshape(DX * I, G * DY),
        "w_pw": a(L0_conv_w_pw).transpose(2, 0, 1).reshape(I, G * I),
        "w_proj": a(L0_conv_w_proj).T,
        "vectors": np.concatenate([a(L0_conv_bn_gamma), a(L0_conv_bn_beta), a(L0_conv_bn_mean), a(L0_conv_bn_var),
                                   a(L0_ffn_bg)]),
        "wg": a(L0_ffn_Wg),
        "w1": a(L0_ffn_W1),
        "b1": a(L0_ffn_b1).reshape(E * KC, 128).T,
        "w2": a(L0_ffn_W2).reshape(E * KC, 128, C).transpose(1, 0, 2).reshape(128, E * KC * C),
        "b2": a(L0_ffn_b2).T,
        "consts": consts,
        "select": select,
    }
    arrays = {f"in_{k}_dram": np.ascontiguousarray(v) for k, v in arrays.items()}
    nc = bacc.Bacc("TRN2", target_bir_lowering=False, num_devices=1)
    args = [nc.dram_tensor(k, v.shape, mybir.dt.from_np(v.dtype), kind="ExternalInput").ap() for k, v in arrays.items()]
    args.append(nc.dram_tensor("out_0_dram", (B, C, H, W), F32, kind="ExternalOutput").ap())
    build(nc, *args)
    r = run_bass_kernel_spmd(nc, [arrays], core_ids=[0])
    return r.results[0]["out_0_dram"]
```

```python
from contextlib import ExitStack

import concourse.bass as bass
from concourse import mybir
import numpy as np

F32 = mybir.dt.float32
F32R = mybir.dt.float32r
ALU = mybir.AluOpType
ACT = mybir.ActivationFunctionType
AX = mybir.AxisListType

B, C, H, W = 8, 64, 16, 16
N = H * W
G, I = 24, 8
QKV = G * I
DY = DX = 5
PAD = DY // 2
YP = H + 2 * PAD
HEADS = 16
HD = HEADS * I
HH = HD // 2
KW = HH + 1
NW = HD + HEADS
E, HID, KC = 8, 256, 2
PAIRS = B // 2
TILES = 4
PT = TILES * 128
GM = 32
GZ = GM * (PAIRS - 1)
GW = 2 * GZ + GM
LN_C_EPS, LN_T_EPS, BN_EPS, ATT_EPS = 1e-6, 1e-5, 1e-5, 1e-15

C_CENTER, C_ONES = 0, 128
C_IDENT = C_ONES + 2
C_HEAD = C_IDENT + 128
C_PAR = C_HEAD + HEADS
C_IOTA = C_PAR + 2
C_END = C_IOTA + E
SELW = (2 * W - 1) * I
LOW = 64


def constants():
    c = np.zeros((128, C_END), np.float32)
    p = np.arange(128)
    half = p // C
    same = half[:, None] == half[None, :]
    c[:, C_CENTER:C_CENTER + 128] = np.eye(128) - same / C
    c[:, C_ONES:C_ONES + 2] = (half[:, None] == np.arange(2)) / C
    c[:, C_IDENT:C_IDENT + 128] = np.eye(128)
    c[:, C_HEAD:C_HEAD + HEADS] = (p // I)[:, None] == np.arange(HEADS)
    c[:, C_PAR:C_PAR + 2] = ((p // H) % 2)[:, None] == np.arange(2)
    c[:, C_IOTA:C_IOTA + E] = np.arange(E)
    s = np.zeros((DX, I, 2 * W - 1, I), np.float32)
    for dx in range(DX):
        for i in range(I):
            s[dx, i, dx - PAD + W - 1, i] = 1
    both = np.zeros((LOW + DX * I, SELW), np.float32)
    both[0:DX * I] = both[LOW:] = s.reshape(DX * I, SELW)
    return c, both


def build(nc, x, w_qkv, w_dw, w_pw, w_proj, vectors, wg, w1, b1, w2, b2, consts, select, out):
    ctx = ExitStack()
    with ctx:
        def sb(name, shape, dt=F32):
            return ctx.enter_context(nc.sbuf_tensor(name, shape, dt))

        def sem(name):
            return ctx.enter_context(nc.semaphore(name))

        X = sb("X", [128, 4 * N])
        CST = sb("CST", [128, C_END])
        SELF = sb("SELF", [LOW + DX * I, SELW])
        WDF = sb("WDF", [LOW + DX * I, G * DY])
        PW = sb("PW", [128, G, I])
        WQ = sb("WQ", [128, 2 * QKV])
        WP = sb("WP", [128, C])
        VEC = sb("VEC", [128, 4 * C + E])
        WG = sb("WG", [128, GW])
        W1 = sb("W1", [128, E * HID])
        B1 = sb("B1", [128, E * KC])
        W2 = sb("W2", [128, E * KC, C])
        B2 = sb("B2", [128, E])
        INV = sb("INV", [128, 2, C])
        BIAS = sb("BIAS", [128, C])
        HALF = sb("HALF", [128, C])
        EULER = sb("EULER", [128, 16])
        EPS1 = sb("EPS1", [128, 1])
        WPS = sb("WPS", [128, 2, C])
        WPM = sb("WPM", [128, 1])
        SEL = sb("SEL", [LOW + DX * I, SELW], F32R)
        WD = sb("WD", [LOW + DX * I, G * DY], F32R)
        WGH, WGL = sb("WGH", [128, GW], F32R), sb("WGL", [128, GW], F32R)
        W1H, W1L = sb("W1H", [128, E * HID], F32R), sb("W1L", [128, E * HID], F32R)
        RS = sb("RS", [128, G, DY, W])
        BAND = sb("BAND", [128, G * DY * 128])
        XC = sb("XC", [128, 4 * N])
        SQ = sb("SQ", [128, 4 * N])
        DEV1 = sb("DEV1", [128, 16])
        NWT = sb("NWT", [128, 3, 16])
        R1 = sb("R1", [128, 8, 2])
        MS = sb("MS", [128, 16, 3 * HD])
        QP = sb("QP", [128, G, YP * B])
        XB = sb("XB", [128, 2, 16, C])
        XBM = sb("XBM", [128, 16])
        SQ2 = sb("SQ2", [128, 2, TILES, C + 1])
        KR = sb("KR", [128, PAIRS, 4, HD])
        VM = sb("VM", [128, PAIRS, 2, 4, 2, KW])
        KV = sb("KV", [128, 2, 2, NW])
        DEN = sb("DEN", [128, 2, TILES, HEADS])
        SM = sb("SM", [128, PAIRS, 2, TILES])
        XS = sb("XS", [128, PAIRS, PT], F32R)
        PLACE = sb("PLACE", [128, 16, E], mybir.dt.uint32)
        GAP = sb("GAP", [128, 5, 16])
        WDN = sb("WDN", [128, PAIRS, 2, 2, E])

        band = BAND[:, :].rearrange("p (g d m) -> p g d m", g=G, d=DY)

        taken = [0]

        def late(*dims):
            first = taken[0]
            taken[0] += int(np.prod(dims))
            assert taken[0] <= G * DY * 128
            names = " ".join("abcde"[:len(dims)])
            return BAND[:, first:taken[0]].rearrange(f"p ({names}) -> p {names}", **dict(zip("abcde", dims)))

        HRING = 4
        hidden = late(HRING, PT)
        QT = late(2, 2, N)
        ATT = late(2, TILES, HD)
        ATTT = late(2, PT)
        X2 = late(8, 2, C)
        XC2 = late(2, TILES, C)
        XN = late(2, TILES, C)
        XHL = late(2, TILES, 2, C)

        LOGITS = late(16, E)
        LARGEST = late(16, E)
        ONEHOT = late(2, 16, E)
        WB = late(2, E, N)
        WIDE = late(E // 2, 2, 2, 2, C)

        outs = XC[:, :].rearrange("p (s n) -> p s n", s=PAIRS)
        GATES = SQ[:, 0:PT]
        WY = SQ[:, PT:PT + 2 * N].rearrange("p (k n) -> p k n", k=2)

        CEN = CST[:, C_CENTER:C_CENTER + 128]
        ONES = CST[:, C_ONES:C_ONES + 2]
        IDT = CST[:, C_IDENT:C_IDENT + 128]
        PAR = CST[:, C_PAR:C_PAR + 2]

        PS = ctx.enter_context(nc.psum_tensor("PS", [128, 8, 512], F32))
        SOFTMAX_PARTS = slice(0, TILES), slice(TILES, PAIRS * TILES)
        CENTER_BANKS, VAR_BANK = (0, 1), 6
        RS_BANK0 = 3
        QKV_RING = (7, 0, 1, 2)
        XT_BANKS = (3, 4)
        CONV_RING = (5, 6, 7, 0)
        LAST_Q_BANK = 1
        CHAIN_BANK = (6, 0, 2, 4)
        Y_BANK0 = 0
        H_RING = (6, 7)
        MISC = (4, 5)
        MISC_USES = 1 + E // 2
        MISC_SLOT = (6,7,8,9,10,11,12,13,14,15,16,17,18,20,21,23,24,26,26,30)

        x_in, centre_in = [sem("x_in_0"), sem("x_in_1")], sem("centre_in")
        cst_in, sel_in, pw_in, wq_in = sem("cst_in"), sem("sel_in"), sem("pw_in"), sem("wq_in")
        vec_in, w1_in, w2_in = sem("vec_in"), sem("w1_in"), sem("w2_in")
        b1_in, b2_in, wp_in = sem("b1_in"), sem("b2_in"), sem("wp_in")
        wq_zero, wg_zero = sem("wq_zero"), sem("wg_zero")
        pads_set = sem("pads_set")
        sel_high, wd_split = sem("sel_high"), sem("wd_split")
        rs_ready, rs_copied, rs_copied_v = sem("rs_ready"), sem("rs_copied"), sem("rs_copied_v")
        centred, xc_ready, sq_ready = sem("centred"), sem("xc_ready"), sem("sq_ready")
        var_ready, dev1_ready, r1_ready = sem("var_ready"), sem("dev1_ready"), sem("r1_ready")
        qkv_ready, scaled_v, scaled_s = sem("qkv_ready"), sem("scaled_v"), sem("scaled_s")
        qp_ready = sem("qp_ready")
        band_v, band_p = sem("band_v"), sem("band_p")
        conv_ready, conv_moved = sem("conv_ready"), sem("conv_moved")
        xt_ready, xb_ready = sem("xt_ready"), sem("xb_ready")
        bn_guarded, inv_ready, wps_ready = sem("bn_guarded"), sem("inv_ready"), sem("wps_ready")
        w_high, w_low = sem("w_high"), sem("w_low")
        ones_set, k_ready, v_ready, v_more = sem("ones_set"), sem("k_ready"), sem("v_ready"), sem("v_more")
        sq2_wanted, sq2_ready = sem("sq2_wanted"), sem("sq2_ready")
        v2_ready, r2_ready, xn_ready = sem("v2_ready"), sem("r2_ready"), sem("xn_ready")
        xh_ready, hi_ready = sem("xh_ready"), sem("hi_ready")
        a_filled, a_read = ([sem(f"a_{k}{s}") for s in range(PAIRS)] for k in ("filled", "read"))
        b_filled, b_read = ([sem(f"b_{k}{s}") for s in range(PAIRS)] for k in ("filled", "read"))
        A_KV, A_NUM, A_ATTT, A_XT = 1, 2, 3, 4
        B_QT, B_NUM, B_PROJ = 1, 2, 3
        gate_ready, gate_read, gates_turned, gates_copied, gap_ready, exp_ready = sem("gate_ready"), sem("gate_read"), sem("gates_turned"), sem("gates_copied"), sem("gap_ready"), sem("exp_ready")
        wdn_ready, wide_ready = sem("wdn_ready"), sem("wide_ready")
        misc_ready, misc_read = sem("misc_ready"), [sem("misc_read_0"), sem("misc_read_1")]
        h_ready, gelu_done, w2_done, y_read = sem("h_ready"), sem("gelu_done"), sem("w2_done"), sem("y_read")
        out_ready, stored = sem("out_ready"), sem("stored")
        v_chain, p_chain = sem("v_chain"), sem("p_chain")

        def by_pixel(k):
            return PS[:, CENTER_BANKS[k], :].rearrange("p (t q r) -> p r q t", q=4, r=4)

        def pair_tokens(t, k):
            return t[:, 512 * k:512 * k + 512].rearrange("p (r q t) -> p r q t", q=4, r=4)

        def qkv_heads(j, h):
            pair, xr = divmod(j, 4)
            return (MS[:, 4 * (2 * h + pair) + xr, 0:3 * HD].rearrange("p (q h i) -> p h q i", q=3, i=I)[:, 0:8],
                    PS[:, QKV_RING[j % 4], QKV * h:QKV * h + QKV].rearrange("p (h q i) -> p h q i", q=3, i=I))

        def head(h):
            return MS[:, :, :].rearrange("p j (q h i) -> p h q j i", q=3, i=I)[:, h]

        def misc_parts(n):
            s, use = divmod(n, MISC_USES)
            if use == 0:
                return outs[:, s, :], PS[:, MISC[n % 2], 0:N]
            return (WB[:, s % 2, 2 * use - 2:2 * use, :].rearrange("p e n -> p (e n)"), PS[:, MISC[n % 2], :])

        def quarter_rs(k):
            return (RS[:, :, :, 4 * k:4 * k + 4].rearrange("p g d x -> p (g d) x"),
                    PS[:, RS_BANK0 + k, 0:480].rearrange("p (x m) -> p m x", x=4))

        def masked_v(s, half, b):
            return (VM[:, s, half, :, b, 0:HH], MS[:, 4 * s:4 * s + 4, 2 * HD + HH * half:2 * HD + HH * half + HH],
                    PAR[:, b:b + 1])

        def y_bank(s, e):
            return Y_BANK0 if s == PAIRS - 1 and e == E - 1 else Y_BANK0 + e // 2

        def widened(s, ep):
            return (WIDE[:, ep].rearrange("p e h b c -> p e (h b) c"),
                    WDN[:, s, :, :, 2 * ep:2 * ep + 2].rearrange("p h b e -> p e (h b)").unsqueeze(3)
                    .broadcast_to([128, 2, 4, C]))

        def band_factors(g):
            return (band[:, g].rearrange("p d (x o) -> p (d x) o", o=I),
                    RS[:, g].rearrange("p d x -> p (d x)").unsqueeze(2).broadcast_to([128, DY * W, I]),
                    PW[:, g, :].unsqueeze(1).broadcast_to([128, DY * W, I]))

        block = ctx.enter_context(nc.Block())

        @block.sync
        def _(sp):
            sp.dma_start(CST[:, 0:C_IDENT], consts[:, 0:C_IDENT]).then_inc(centre_in, 16)
            sp.dma_start(X[:, 2 * N:4 * N], x[:, 2 * N:4 * N]).then_inc(x_in[1], 16)
            sp.wait_ge(wq_zero, 1)
            for h in range(2):
                sp.dma_start(WQ[C * h:C * h + C, QKV * h:QKV * h + QKV], w_qkv).then_inc(wq_in, 16)
            sp.dma_start(CST[:, C_IDENT:C_END], consts[:, C_IDENT:C_END]).then_inc(cst_in, 16)
            sp.dma_start(VEC[:, :], vectors.unsqueeze(0).broadcast_to([128, 4 * C + E])).then_inc(vec_in, 16)
            sp.dma_start(PW[:, :, :].rearrange("p g o -> p (g o)"),
                         w_pw.unsqueeze(0).broadcast_to([W, I, QKV])).then_inc(pw_in, 16)
            sp.dma_start(WP[:, :], w_proj).then_inc(wp_in, 16)
            sp.wait_ge(wg_zero, 1)
            for h in range(2):
                sp.dma_start(WG[C * h:C * h + C, GZ:GZ + E], wg).then_inc(w1_in, 16)
                sp.dma_start(W1[C * h:C * h + C, :].rearrange("c (e n) -> c e n", e=E),
                             w1.rearrange("e c n -> c e n")).then_inc(w1_in, 16)
            sp.dma_start(W2[:, :, :].rearrange("p k c -> p (k c)"), w2).then_inc(w2_in, 16)
            sp.dma_start(B1[:, :], b1).then_inc(b1_in, 16)
            for h in range(2):
                sp.dma_start(B2[C * h:C * h + C, :], b2).then_inc(b2_in, 16)
            for s in range(PAIRS):
                sp.wait_ge(out_ready, s + 1)
                sp.dma_start(out[2 * s:2 * s + 2].rearrange("b c y x -> (b c) (y x)"), outs[:, s, :]).then_inc(stored, 16)
            sp.wait_ge(stored, 16 * PAIRS)

        @block.gpsimd
        def _(pool):
            pool.memset(WQ[:, :], 0.0).then_inc(wq_zero, 1)
            pool.memset(WG[:, :], 0.0).then_inc(wg_zero, 1)
            pool.memset(EPS1[:, :], LN_C_EPS).then_inc(pads_set, 1)
            pool.memset(HALF[:, :], -0.5).then_inc(pads_set, 1)
            pool.memset(EULER[:, :], float(np.e)).then_inc(pads_set, 1)
            pool.memset(QP[:, :, 0:PAD * B], 0.0).then_inc(pads_set, 1)
            pool.memset(QP[:, :, (PAD + H) * B:YP * B], 0.0).then_inc(pads_set, 1)
            pool.memset(SQ2[:, :, :, C:C + 1], LN_T_EPS).then_inc(pads_set, 1)
            pool.memset(KV[:, :, :, :], 0.0).then_inc(pads_set, 1)
            pool.wait_ge(pads_set, 7)
            pool.wait_ge(cst_in, 16)
            pool.tensor_copy(VM[:, :, :, :, :, HH].rearrange("p s h r b -> p (s h r) b"),
                             PAR.unsqueeze(1).broadcast_to([128, 8 * PAIRS, 2])).then_inc(ones_set, 1)
            pool.wait_ge(vec_in, 16)
            pool.tensor_scalar(INV[:, 0, :], VEC[:, 3 * C:4 * C], BN_EPS, None, ALU.add).then_inc(bn_guarded, 1)
            pool.wait_ge(bn_guarded, 1)
            pool.tensor_tensor(INV[:, 1, :], INV[:, 0, :], HALF[:, :], ALU.pow).then_inc(inv_ready, 1)
            pool.wait_ge(rs_copied, 2)
            pool.wait_ge(rs_copied_v, 2)
            pool.wait_ge(pw_in, 16)
            for g in range(2, G, 3):
                pool.tensor_tensor(*band_factors(g), ALU.mult).then_inc(band_p, 1)
            pool.wait_ge(w_high, 2)
            pool.tensor_tensor(W1L[:, :], W1[:, :], W1H[:, :].bitcast(F32), ALU.subtract).then_inc(w_low, 1)
            pool.tensor_tensor(WGL[:, :], WG[:, :], WGH[:, :].bitcast(F32), ALU.subtract).then_inc(w_low, 1)
            pool.wait_ge(conv_moved, 8)
            for s in range(1, PAIRS):
                for b in range(2):
                    pool.tensor_scalar(*masked_v(s, 1, b), None, ALU.mult).then_inc(v_more, 1)
            for s in range(PAIRS):
                pool.wait_ge(v2_ready, s + 1)
                pool.tensor_tensor(SM[:, s, 1, :], SM[:, s, 0, :], HALF[:, 0:TILES], ALU.pow).then_inc(r2_ready, 1)
            for part, tiles in enumerate(SOFTMAX_PARTS):
                pool.wait_ge(gap_ready, part + 1)
                pool.tensor_tensor(GAP[:, 1, tiles], EULER[:, tiles], GAP[:, 0, tiles], ALU.pow).then_inc(exp_ready, 1)
            pool.wait_ge(wdn_ready, 4)
            pool.wait_ge(wide_ready, E // 2)
            for s in range(1, PAIRS):
                for ep in range(E // 2):
                    pool.wait_ge(misc_ready, MISC_USES * (s - 1) + 2 + ep)
                    pool.tensor_copy(*widened(s, ep)).then_inc(wide_ready, 1)

        @block.scalar
        def _(act):
            act.dma_start(X[:, 0:2 * N], x[:, 0:2 * N]).then_inc(x_in[0], 16)
            act.dma_start(WDF[:, :], w_dw).then_inc(sel_in, 16)
            act.dma_start(SELF[:, :], select).then_inc(sel_in, 16)
            act.preload_act_table(ACT.Sqrt)
            act.wait_ge(sel_in, 32)
            act.activation(SEL[:, :], SELF[:, :], ACT.Copy).then_inc(sel_high, 1)
            for k in range(2):
                act.wait_ge(xc_ready, k + 1)
                act.activation(SQ[:, 512 * k:512 * k + 512], XC[:, 512 * k:512 * k + 512], ACT.Square).then_inc(sq_ready, 1)
            act.wait_ge(var_ready, 1)
            act.wait_ge(pads_set, 7)
            act.activation(DEV1[:, :], PS[:, VAR_BANK, 0:16], ACT.Sqrt, bias=EPS1[:, :]).then_inc(dev1_ready, 1)
            act.wait_ge(r1_ready, 1)

            def scale_qkv(j):
                act.wait_ge(qkv_ready, j + 1)
                for h in range(2):
                    to, of = qkv_heads(j, h)
                    i = act.activation(to, of, ACT.Copy, scale=R1[:, j, h:h + 1])
                i.then_inc(scaled_s, 1)

            def copy_rs(k):
                act.wait_ge(rs_ready, k + 1)
                act.activation(*quarter_rs(k), ACT.Copy).then_inc(rs_copied, 1)

            scale_qkv(1)
            scale_qkv(3)
            copy_rs(0)
            copy_rs(2)
            scale_qkv(5)
            scale_qkv(7)
            act.preload_act_table(ACT.Gelu)
            act.wait_ge(w1_in, 64)
            act.activation(W1H[:, :], W1[:, :], ACT.Copy).then_inc(w_high, 1)
            act.activation(WGH[:, :], WG[:, :], ACT.Copy).then_inc(w_high, 1)

            def relu_k(s, half):
                act.activation(KR[:, s, :, HH * half:HH * half + HH],
                               MS[:, 4 * s:4 * s + 4, HD + HH * half:HD + HH * half + HH], ACT.Relu).then_inc(k_ready, 1)

            act.wait_ge(scaled_v, 4)
            act.wait_ge(scaled_s, 4)
            act.wait_ge(cst_in, 16)
            for s in range(PAIRS):
                relu_k(s, 0)
                for b in range(2):
                    to, of, one = masked_v(s, 0, b)
                    act.activation(to, of, ACT.Copy, scale=one)
            act.wait_ge(conv_moved, 8)

            def relu_qt(s):
                act.wait_ge(b_filled[s], B_QT)
                if s >= 2:
                    act.wait_ge(b_filled[s - 2], B_NUM)
                for b in range(2):
                    i = act.activation(
                        QT[:, s % 2, b, :].rearrange("p (y q r) -> p r q y", q=4, r=4),
                        PS[:, CHAIN_BANK[s] + 1, :].rearrange("p (r q b y) -> p b r q y", r=4, q=4, b=2)[:, b],
                        ACT.Relu)
                i.then_inc(b_read[s], 1)

            def copy_attt(s):
                act.wait_ge(a_filled[s], A_ATTT)
                if s >= 2:
                    act.wait_ge(b_filled[s - 2], B_PROJ)
                act.activation(ATTT[:, s % 2, :], PS[:, CHAIN_BANK[s], :], ACT.Copy).then_inc(a_read[s], 1)

            def square_xc(s):
                act.wait_ge(sq2_wanted, s + 1)
                if s >= 2:
                    act.wait_ge(v2_ready, s - 1)
                act.activation(SQ2[:, s % 2, :, 0:C], XC2[:, s % 2], ACT.Square, scale=C ** -0.5).then_inc(sq2_ready, 1)

            def high(s):
                act.wait_ge(xn_ready, s + 1)
                if s >= 2:
                    act.wait_ge(a_filled[s - 2], A_XT)
                act.activation(XHL[:, s % 2, :, 0, :].bitcast(F32R), XN[:, s % 2], ACT.Copy).then_inc(hi_ready, 1)

            def copy_xs(s):
                act.wait_ge(a_filled[s], A_XT)
                act.activation(XS[:, s, :], PS[:, CHAIN_BANK[s], :], ACT.Copy).then_inc(a_read[s], 1)

            def read_misc(n):
                to, of = misc_parts(n)
                act.wait_ge(misc_ready, n + 1)
                s, use = divmod(n, MISC_USES)
                if s >= 2 and use >= 1:
                    act.wait_ge(y_read, E * (s - 2) + 2 * use)
                act.activation(to, of, ACT.Copy).then_inc(misc_read[n % 2], 1)

            def gelu(s, e):
                for k in range(KC * e, KC * e + KC):
                    n = KC * E * s + k
                    act.wait_ge(h_ready, n + 1)
                    if n >= HRING:
                        act.wait_ge(w2_done, n // KC - 1)
                    act.activation(hidden[:, n % HRING, :], PS[:, H_RING[n % 2], :], ACT.Gelu,
                                   bias=B1[:, k:k + 1]).then_inc(gelu_done, 1)

            act.wait_ge(b1_in, 16)
            relu_k(0, 1)
            relu_k(1, 1)
            relu_k(2, 1)
            relu_k(3, 1)
            relu_qt(0)
            relu_qt(1)
            copy_attt(0)
            relu_qt(2)
            relu_qt(3)
            square_xc(0)
            copy_attt(1)
            copy_attt(2)
            square_xc(1)
            high(0)
            copy_xs(0)
            high(1)
            gelu(0, 0)
            copy_xs(1)
            square_xc(2)
            gelu(0, 1)
            copy_attt(3)
            gelu(0, 2)
            high(2)
            square_xc(3)
            gelu(0, 3)
            copy_xs(2)
            high(3)
            gelu(0, 4)
            copy_xs(3)
            for s in range(PAIRS):
                for e in range(5 if s == 0 else 0, E):
                    gelu(s, e)
                    for n in range(MISC_USES * PAIRS):
                        if MISC_SLOT[n] == E * s + e:
                            read_misc(n)

        @block.vector
        def _(dve):
            chain = [0]

            def link(i):
                chain[0] += 1
                i.then_inc(v_chain, 1)
                dve.wait_ge(v_chain, chain[0])

            def bands(g):
                dve.tensor_tensor(*band_factors(g), ALU.mult).then_inc(band_v, 1)

            dve.wait_ge(sel_in, 32)
            link(dve.tensor_copy(WD[:, :], WDF[:, :]))
            dve.tensor_tensor(WD[LOW:LOW + DX * I, :], WDF[LOW:LOW + DX * I, :], WD[LOW:LOW + DX * I, :].bitcast(F32),
                              ALU.subtract).then_inc(wd_split, 1)
            for k in range(2):
                dve.wait_ge(centred, k + 1)
                dve.tensor_copy(pair_tokens(XC, k), by_pixel(k)).then_inc(xc_ready, 1)
            dve.wait_ge(dev1_ready, 1)
            link(dve.reciprocal(NWT[:, 0, :], DEV1[:, :]))
            link(dve.scalar_tensor_tensor(out=NWT[:, 1, :], in0=PS[:, VAR_BANK, 0:16], scalar=LN_C_EPS, in1=NWT[:, 0, :],
                                          op0=ALU.add, op1=ALU.mult))
            link(dve.scalar_tensor_tensor(out=NWT[:, 2, :], in0=NWT[:, 1, :], scalar=-0.5, in1=NWT[:, 0, :],
                                          op0=ALU.mult, op1=ALU.mult))
            dve.scalar_tensor_tensor(out=R1[:, :, :].rearrange("p j h -> p (j h)"), in0=NWT[:, 2, :], scalar=1.5,
                                     in1=NWT[:, 0, :], op0=ALU.add, op1=ALU.mult).then_inc(r1_ready, 1)
            dve.wait_ge(r1_ready, 1)

            def scale_qkv(j):
                dve.wait_ge(qkv_ready, j + 1)
                for h in range(2):
                    to, of = qkv_heads(j, h)
                    i = dve.tensor_scalar(to, of, R1[:, j, h:h + 1], None, ALU.mult)
                i.then_inc(scaled_v, 1)

            def copy_rs(k):
                dve.wait_ge(rs_ready, k + 1)
                dve.tensor_copy(*quarter_rs(k)).then_inc(rs_copied_v, 1)

            scale_qkv(0)
            scale_qkv(2)
            copy_rs(1)
            scale_qkv(4)
            copy_rs(3)
            scale_qkv(6)
            dve.wait_ge(rs_copied, 2)
            dve.wait_ge(rs_copied_v, 2)
            dve.wait_ge(pw_in, 16)
            bands(0)
            dve.wait_ge(scaled_v, 4)
            dve.wait_ge(scaled_s, 4)
            dve.wait_ge(pads_set, 7)
            qp = QP[:, :, :].rearrange("p g (y b) -> p g b y", b=B)

            def move_head(h):
                dve.wait_ge(conv_ready, h + 1)
                of = PS[:, CONV_RING[h % 4], 0:3 * 128].rearrange("p (q y b) -> p q b y", q=3, b=B)
                if h < 7:
                    dve.transpose(head(8 + h), of).then_inc(conv_moved, 1)
                else:
                    dve.transpose(head(8 + h)[:, 1:3], of[:, 1:3]).then_inc(conv_moved, 1)

            def move_last_q():
                dve.wait_ge(conv_ready, 9)
                dve.transpose(head(15)[:, 0], PS[:, LAST_Q_BANK, 0:128].rearrange("p (y b) -> p b y", b=B))\
                    .then_inc(conv_moved, 1)

            for h in range(8):
                dve.transpose(qp[:, 3 * h:3 * h + 3, :, PAD:PAD + H], head(h)).then_inc(qp_ready, 1)
                if h == 0:
                    bands(1)
                else:
                    bands(3 * h)
                    bands(3 * h + 1)
                if h >= 3:
                    move_head(h - 3)
                if h == 5:
                    dve.wait_ge(inv_ready, 1)
                    dve.wait_ge(vec_in, 16)
                    dve.wait_ge(wp_in, 16)
                    link(dve.tensor_tensor(INV[:, 0, :], INV[:, 1, :], VEC[:, 0:C], ALU.mult))
                    link(dve.tensor_tensor(BIAS[:, :], VEC[:, 2 * C:3 * C], INV[:, 0, :], ALU.mult))
                    link(dve.tensor_tensor(BIAS[:, :], VEC[:, C:2 * C], BIAS[:, :], ALU.subtract))
                    link(dve.tensor_tensor(WPS[:, 0, :], WP[:, :], INV[:, 0, :], ALU.mult))
                    link(dve.tensor_reduce(WPM[:, :], WPS[:, 0, :], AX.X, ALU.add))
                    dve.scalar_tensor_tensor(out=WPS[:, 1, :], in0=WPM[:, :].broadcast_to([128, C]), scalar=-1.0 / C,
                                             in1=WPS[:, 0, :], op0=ALU.mult, op1=ALU.add).then_inc(wps_ready, 1)
                if h == 6:
                    for k in range(2):
                        dve.wait_ge(xt_ready, k + 1)
                        i = dve.tensor_tensor(
                            XB[:, 0, :, :].rearrange("p (h t) c -> p t h c", h=2)[:, 4 * k:4 * k + 4],
                            PS[:, XT_BANKS[k], :].rearrange("p (t h c) -> p t h c", t=4, h=2),
                            BIAS[:, :].unsqueeze(1).unsqueeze(1).broadcast_to([128, 4, 2, C]), ALU.add)
                        i.then_inc(xb_ready, 1)
                if h == 7:
                    dve.wait_ge(xb_ready, 2)
                    link(dve.tensor_reduce(XBM[:, :], XB[:, 0, :, :], AX.X, ALU.add))
                    link(dve.scalar_tensor_tensor(out=XB[:, 1, :, :], in0=XBM[:, :].unsqueeze(2).broadcast_to([128, 16, C]),
                                                  scalar=-1.0 / C, in1=XB[:, 0, :, :], op0=ALU.mult, op1=ALU.add))
            move_head(5)
            move_head(6)
            move_head(7)
            dve.wait_ge(conv_moved, 8)

            def read_kv(s):
                dve.wait_ge(a_filled[s], A_KV)
                if s >= 2:
                    dve.wait_ge(b_filled[s - 2], B_NUM)
                kv = PS[:, CHAIN_BANK[s], 0:2 * KW].rearrange("p (b v) -> p b v", b=2)
                own = CST[:, C_HEAD:C_HEAD + HEADS].unsqueeze(1)
                for half in range(2):
                    rows, heads = slice(HH * half, HH * half + HH), slice(8 * half, 8 * half + 8)
                    dve.tensor_tensor(KV[rows, s % 2, :, rows].rearrange("p b (h v) -> p b h v", v=I),
                                      kv[rows, :, 0:HH].rearrange("p b (h v) -> p b h v", v=I),
                                      own[rows, :, heads].unsqueeze(3).broadcast_to([HH, 2, 8, I]), ALU.mult)
                dve.tensor_tensor(KV[:, s % 2, :, HD:NW], kv[:, :, HH:KW].broadcast_to([128, 2, HEADS]),
                                  own.broadcast_to([128, 2, HEADS]), ALU.mult).then_inc(a_read[s], 1)

            def attend(s):
                dve.wait_ge(a_filled[s], A_NUM)
                dve.wait_ge(b_filled[s], B_NUM)
                nd = PS[:, CHAIN_BANK[s]:CHAIN_BANK[s] + 2, 0:2 * NW].rearrange("p k (t v) -> p k t v", t=2)
                link(dve.tensor_scalar(DEN[:, 0, :, :].rearrange("p (k t) h -> p k t h", k=2), nd[:, :, :, HD:NW],
                                       ATT_EPS, None, ALU.add))
                link(dve.reciprocal(DEN[:, 1, :, :].rearrange("p t h -> p (t h)"),
                                    DEN[:, 0, :, :].rearrange("p t h -> p (t h)")))
                if s >= 2:
                    dve.wait_ge(a_filled[s - 2], A_ATTT)
                for k, read in enumerate((a_read[s], b_read[s])):
                    dve.tensor_tensor(
                        ATT[:, s % 2, 2 * k:2 * k + 2, :].rearrange("p t (h v) -> p t h v", v=I),
                        nd[:, k, :, 0:HD].rearrange("p t (h v) -> p t h v", v=I),
                        DEN[:, 1, 2 * k:2 * k + 2, :].unsqueeze(3).broadcast_to([128, 2, HEADS, I]), ALU.mult)\
                        .then_inc(read, 1)

            def residual(s):
                dve.wait_ge(b_filled[s], B_PROJ)
                both = PS[:, CHAIN_BANK[s] + 1, :].rearrange("p (t k c) -> p k t c", t=TILES, k=2)
                if s >= 2:
                    dve.wait_ge(xn_ready, s - 1)
                dve.tensor_tensor(XC2[:, s % 2], both[:, 1], XB[:, 1, TILES * s:TILES * s + TILES, :], ALU.add)\
                    .then_inc(sq2_wanted, 1)
                dve.tensor_tensor(X2[:, 2 * s:2 * s + 2].rearrange("p h b c -> p b h c"),
                                  both[:, 0].rearrange("p (b h) c -> p b h c", b=2),
                                  XB[:, 0, TILES * s:TILES * s + TILES, :].rearrange("p (b h) c -> p b h c", b=2),
                                  ALU.add).then_inc(b_read[s], 1)

            def variance(s):
                dve.wait_ge(sq2_ready, s + 1)
                dve.tensor_reduce(SM[:, s, 0, :], SQ2[:, s % 2], AX.X, ALU.add).then_inc(v2_ready, 1)

            def scale(s):
                dve.wait_ge(r2_ready, s + 1)
                dve.wait_ge(sq2_wanted, s + 1)
                if s >= 2:
                    dve.wait_ge(xh_ready, s - 1)
                dve.tensor_tensor(XN[:, s % 2], XC2[:, s % 2],
                                  SM[:, s, 1, :].unsqueeze(2).broadcast_to([128, TILES, C]), ALU.mult).then_inc(xn_ready, 1)

            def low(s):
                dve.wait_ge(xn_ready, s + 1)
                dve.wait_ge(hi_ready, s + 1)
                dve.tensor_tensor(XHL[:, s % 2, :, 1, :].bitcast(F32R), XN[:, s % 2], XHL[:, s % 2, :, 0, :],
                                  ALU.subtract).then_inc(xh_ready, 1)

            def copy_gates():
                dve.wait_ge(gate_ready, 1)
                dve.tensor_copy(GATES[:, :], PS[:, MISC[0], :]).then_inc(gates_copied, 1)

            def read_gates():
                dve.wait_ge(gates_turned, 1)
                dve.tensor_tensor(LOGITS[:, :, :].rearrange("p (s t) e -> p s t e", t=TILES),
                                  PS[:, MISC[1], :].rearrange("p (t s e) -> p s t e", t=TILES, e=GM)[:, :, :, 0:E],
                                  VEC[:, 4 * C:4 * C + E].unsqueeze(1).unsqueeze(1).broadcast_to([128, PAIRS, TILES, E]),
                                  ALU.add).then_inc(gate_read, 1)
                dve.wait_ge(gate_read, 1)

            def top2(part):
                tiles = SOFTMAX_PARTS[part]
                for t in range(tiles.start, tiles.stop):
                    i = dve.max(LARGEST[:, t, :], LOGITS[:, t, :])
                link(i)
                dve.tensor_tensor(GAP[:, 0, tiles], LARGEST[:, tiles, 1], LARGEST[:, tiles, 0], ALU.subtract).then_inc(gap_ready, 1)
                for t in range(tiles.start, tiles.stop):
                    i = dve.max_index(PLACE[:, t, :], LARGEST[:, t, :], LOGITS[:, t, :])
                link(i)
                for k in range(2):
                    i = dve.tensor_tensor(ONEHOT[:, k, tiles, :],
                                          CST[:, C_IOTA:C_IOTA + E].unsqueeze(1).broadcast_to([128, tiles.stop - tiles.start, E]),
                                          PLACE[:, tiles, k:k + 1].broadcast_to([128, tiles.stop - tiles.start, E]),
                                          ALU.is_equal)
                link(i)

            def softmax(part):
                tiles, pairs = SOFTMAX_PARTS[part], slice(0, 1) if part == 0 else slice(1, PAIRS)
                O1, O2 = ONEHOT[:, 0, tiles], ONEHOT[:, 1, tiles]
                ex, dn, q1, q2 = (GAP[:, k, tiles] for k in (1, 2, 3, 4))

                def wide(v):
                    return v.unsqueeze(2).broadcast_to([128, tiles.stop - tiles.start, E])

                dve.wait_ge(exp_ready, part + 1)
                link(dve.tensor_scalar(dn, ex, 1.0, None, ALU.add))
                link(dve.reciprocal(q1, dn))
                link(dve.tensor_tensor(q2, ex, q1, ALU.mult))
                dve.tensor_tensor(O1, O1, wide(q1), ALU.mult)
                link(dve.tensor_tensor(O2, O2, wide(q2), ALU.mult))
                for b in range(2):
                    dve.tensor_tensor(WDN[:, pairs, :, b, :], O1.rearrange("p (s b h) e -> p b s h e", b=2, h=2)[:, b],
                                      O2.rearrange("p (s b h) e -> p b s h e", b=2, h=2)[:, b], ALU.add).then_inc(wdn_ready, 1)

            def widen(ep):
                dve.wait_ge(wdn_ready, 2)
                dve.tensor_copy(*widened(0, ep)).then_inc(wide_ready, 1)

            def combine(s, ep):
                for n in (MISC_USES * s, MISC_USES * s + 1 + ep):
                    dve.wait_ge(misc_read[n % 2], n // 2 + 1)
                if s >= 1 and ep == 0:
                    dve.wait_ge(out_ready, s)

                def weigh(e):
                    dve.scalar_tensor_tensor(out=WY[:, e % 2, :], in0=PS[:, y_bank(s, e), N * (e % 2):N * (e % 2) + N],
                                             scalar=B2[:, e:e + 1], in1=WB[:, s % 2, e, :], op0=ALU.add, op1=ALU.mult)\
                        .then_inc(y_read, 1)

                def add_up(e):
                    dve.wait_ge(y_read, E * s + e + 1)
                    i = dve.tensor_tensor(outs[:, s, :], outs[:, s, :], WY[:, e % 2, :], ALU.add)
                    if e == E - 1:
                        i.then_inc(out_ready, 1)
                    else:
                        link(i)

                if y_bank(s, 2 * ep) == y_bank(s, 2 * ep + 1):
                    dve.wait_ge(w2_done, E * s + 2 * ep + 2)
                    weigh(2 * ep)
                    weigh(2 * ep + 1)
                    add_up(2 * ep)
                    add_up(2 * ep + 1)
                else:
                    for e in range(2 * ep, 2 * ep + 2):
                        dve.wait_ge(w2_done, E * s + e + 1)
                        weigh(e)
                        add_up(e)

            for b in range(2):
                dve.tensor_scalar(*masked_v(0, 1, b), None, ALU.mult).then_inc(v_ready, 1)
            move_last_q()
            read_kv(0)
            read_kv(1)
            attend(0)
            read_kv(2)
            attend(1)
            residual(0)
            attend(2)
            variance(0)
            read_kv(3)
            residual(1)
            scale(0)
            variance(1)
            low(0)
            scale(1)
            residual(2)
            low(1)
            attend(3)
            variance(2)
            scale(2)
            residual(3)
            variance(3)
            low(2)
            scale(3)
            low(3)
            copy_gates()
            read_gates()
            top2(0)
            softmax(0)
            widen(0)
            widen(1)
            widen(2)
            dve.wait_ge(b2_in, 32)
            for s in range(PAIRS):
                for ep in range(E // 2):
                    combine(s, ep)
                    if s == 0 and ep == 0:
                        top2(1)
                        widen(3)
                        softmax(1)

        @block.tensor
        def _(pe):
            def mm(bank, cols, lhsT, rhs, start, stop, parts=128):
                return pe.matmul(PS[0:parts, bank, cols[0]:cols[1]], lhsT, rhs, start=start, stop=stop)

            pe.wait_ge(centre_in, 16)
            for k in range(2):
                pe.wait_ge(x_in[k], 16)
                mm(CENTER_BANKS[k], (0, 512), CEN, X[:, 512 * k:512 * k + 512], True, True).then_inc(centred, 1)
            pe.wait_ge(wq_in, 32)

            def qkv(j):
                pe.wait_ge(xc_ready, 1 if j < 4 else 2)
                if j >= 4:
                    pe.wait_ge(scaled_s if j % 2 else scaled_v, (j - 4) // 2 + 1)
                elif QKV_RING[j] == CENTER_BANKS[1]:
                    pe.wait_ge(xc_ready, 2)
                mm(QKV_RING[j % 4], (0, 2 * QKV), XC[:, 128 * j:128 * j + 128], WQ[:, :], True, True).then_inc(qkv_ready, 1)

            for j in range(4):
                qkv(j)
            pe.wait_ge(sq_ready, 2)
            for j in range(8):
                i = mm(VAR_BANK, (2 * j, 2 * j + 2), SQ[:, 128 * j:128 * j + 128], ONES, True, True)
            i.then_inc(var_ready, 1)
            pe.wait_ge(sel_high, 1)
            pe.wait_ge(wd_split, 1)
            for k in range(4):
                if RS_BANK0 + k == VAR_BANK:
                    pe.wait_ge(r1_ready, 1)
                for j in range(4):
                    xo = 4 * k + j
                    i = mm(RS_BANK0 + k, (120 * j, 120 * j + 120), SEL[:, (W - 1 - xo) * I:(W - 1 - xo) * I + 128],
                           WD[:, :], True, True)
                i.then_inc(rs_ready, 1)
            for j in range(4, 8):
                qkv(j)
            pe.wait_ge(cst_in, 16)
            pe.wait_ge(rs_copied, 2)
            pe.wait_ge(rs_copied_v, 2)
            for t in range(8):
                i = pe.transpose(PS[:, XT_BANKS[t // 4], 128 * (t % 4):128 * (t % 4) + 128],
                                 X[:, 128 * t:128 * t + 128], IDT)
                if t % 4 == 3:
                    i.then_inc(xt_ready, 1)
            pe.wait_ge(scaled_v, 4)
            pe.wait_ge(scaled_s, 4)
            for h in range(8):
                pe.wait_ge(qp_ready, h + 1)
                if h >= 4:
                    pe.wait_ge(conv_moved, h - 3)
                for q in (1, 2, 0) if h == 7 else (0, 1, 2):
                    bank = LAST_Q_BANK if h == 7 and q == 0 else CONV_RING[h % 4]
                    if q < 2:
                        pe.wait_ge(band_v, 2 * h + q + 1)
                    else:
                        pe.wait_ge(band_p, h + 1)
                    for dy in range(DY):
                        i = mm(bank, (128 * q, 128 * q + 128), band[:, 3 * h + q, dy, :],
                               QP[:, 3 * h + q, dy * B:dy * B + 128], dy == 0, dy == DY - 1)
                    if q == 2:
                        i.then_inc(conv_ready, 1)
            i.then_inc(conv_ready, 1)

            def kv(s):
                pe.wait_ge(k_ready, PAIRS + s + 1)
                if s == 0:
                    pe.wait_ge(v_ready, 2)
                    pe.wait_ge(ones_set, 1)
                else:
                    pe.wait_ge(v_more, 2 * s)
                for r in range(4):
                    for half in range(2):
                        rows = slice(HH * half, HH * half + HH)
                        i = pe.matmul(PS[rows, CHAIN_BANK[s], 0:2 * KW], KR[:, s, r, rows],
                                      VM[:, s, half, r].rearrange("p b v -> p (b v)"), start=r == 0, stop=r == 3)
                i.then_inc(a_filled[s], 1)

            def qt(s):
                for r in range(4):
                    i = pe.transpose(PS[:, CHAIN_BANK[s] + 1, 128 * r:128 * r + 128], MS[:, 4 * s + r, 0:HD], IDT)
                i.then_inc(b_filled[s], 1)

            def num(s):
                pe.wait_ge(a_read[s], A_KV)
                pe.wait_ge(b_read[s], B_QT)
                for t in range(TILES):
                    i = mm(CHAIN_BANK[s] + t // 2, (NW * (t % 2), NW * (t % 2) + NW),
                           QT[:, s % 2, t // 2, 128 * (t % 2):128 * (t % 2) + 128], KV[:, s % 2, t // 2, :], True, True)
                    if t == 1:
                        i.then_inc(a_filled[s], 1)
                i.then_inc(b_filled[s], 1)

            def attt(s):
                pe.wait_ge(a_read[s], A_NUM)
                pe.wait_ge(b_read[s], B_NUM)
                for t in range(TILES):
                    i = pe.transpose(PS[:, CHAIN_BANK[s], 128 * t:128 * t + 128], ATT[:, s % 2, t, :], IDT)
                i.then_inc(a_filled[s], 1)

            def proj(s):
                pe.wait_ge(a_read[s], A_ATTT)
                pe.wait_ge(wps_ready, 1)
                for t in range(TILES):
                    i = mm(CHAIN_BANK[s] + 1, (128 * t, 128 * t + 128), ATTT[:, s % 2, 128 * t:128 * t + 128],
                           WPS[:, :, :].rearrange("p k c -> p (k c)"), True, True)
                i.then_inc(b_filled[s], 1)

            def xt(s):
                pe.wait_ge(xh_ready, s + 1)
                for t in range(TILES):
                    i = pe.transpose(PS[:, CHAIN_BANK[s], 128 * t:128 * t + 128],
                                     XHL[:, s % 2, t].rearrange("p k c -> p (k c)"), IDT)
                i.then_inc(a_filled[s], 1)

            def gate():
                for s in range(PAIRS):
                    pe.wait_ge(a_read[s], A_XT)
                for s in range(PAIRS):
                    for k, w in enumerate((WGH, WGL)):
                        i = pe.matmul(PS[:, MISC[0], :], w[:, GZ - GM * s:GZ - GM * s + 128], XS[:, s, :],
                                      start=s == k == 0, stop=s == PAIRS - 1 and k == 1)
                i.then_inc(gate_ready, 1)

            def turn_gates():
                pe.wait_ge(gates_copied, 1)
                pe.wait_ge(b_read[PAIRS - 1], B_PROJ)
                for t in range(TILES):
                    i = pe.transpose(PS[:, MISC[1], 128 * t:128 * t + 128], GATES[:, 128 * t:128 * t + 128], IDT)
                i.then_inc(gates_turned, 1)

            def tokens(s):
                n = MISC_USES * s
                if n >= 2:
                    pe.wait_ge(misc_read[n % 2], n // 2)
                else:
                    pe.wait_ge(gate_read, 1)
                for half in range(2):
                    i = pe.transpose(PS[:, MISC[n % 2], 128 * half:128 * half + 128],
                                     X2[:, 2 * s + half].rearrange("p b c -> p (b c)"), IDT)
                i.then_inc(misc_ready, 1)

            def weights(s, ep):
                n = MISC_USES * s + 1 + ep
                if n >= 2:
                    pe.wait_ge(misc_read[n % 2], n // 2)
                pe.wait_ge(wide_ready, E // 2 * s + ep + 1)
                for e in range(2):
                    for half in range(2):
                        i = pe.transpose(PS[:, MISC[n % 2], N * e + 128 * half:N * e + 128 * half + 128],
                                         WIDE[:, ep, e, half].rearrange("p b c -> p (b c)"), IDT)
                i.then_inc(misc_ready, 1)

            def first_layer(s, e):
                pe.wait_ge(a_read[s], A_XT)
                if s == e == 0:
                    pe.wait_ge(b_read[0], B_PROJ)
                    pe.wait_ge(w_low, 2)
                for k in range(KC * e, KC * e + KC):
                    n = KC * E * s + k
                    if n >= 2:
                        pe.wait_ge(gelu_done, n - 1)
                    for m, w in enumerate((W1H, W1L)):
                        i = mm(H_RING[n % 2], (0, PT), w[:, 128 * k:128 * k + 128], XS[:, s, :], m == 0, m == 1)
                    i.then_inc(h_ready, 1)

            def second_layer(s, e):
                pe.wait_ge(gelu_done, KC * (E * s + e) + KC)
                if y_bank(s, e) != Y_BANK0 + e // 2:
                    pe.wait_ge(y_read, E * s + 2)
                elif s >= 1:
                    pe.wait_ge(y_read, E * (s - 1) + 2 * (e // 2) + 2)
                if s == 0 and e % 4 == 0:
                    owner = 1 + e // 4
                    pe.wait_ge(a_read[owner], A_XT)
                    pe.wait_ge(b_read[owner], B_PROJ)
                if s == e == 0:
                    pe.wait_ge(w2_in, 16)
                for k in range(KC):
                    for b in range(2):
                        i = pe.matmul(PS[C * b:C * b + C, y_bank(s, e), N * (e % 2):N * (e % 2) + N],
                                      W2[:, KC * e + k, :], hidden[:, (KC * (E * s + e) + k) % HRING, N * b:N * b + N],
                                      start=k == 0, stop=k == KC - 1)
                i.then_inc(w2_done, 1)

            pe.wait_ge(conv_moved, 8)
            pe.wait_ge(xb_ready, 2)
            kv(0)
            pe.wait_ge(conv_moved, 9)
            qt(0)
            qt(1)
            kv(1)
            num(0)
            kv(2)
            num(1)
            attt(0)
            qt(2)
            qt(3)
            proj(0)
            num(2)
            kv(3)
            attt(1)
            proj(1)
            attt(2)
            num(3)
            proj(2)
            xt(0)
            first_layer(0, 0)
            xt(1)
            first_layer(0, 1)
            second_layer(0, 0)
            attt(3)
            first_layer(0, 2)
            proj(3)
            second_layer(0, 1)
            first_layer(0, 3)
            second_layer(0, 2)
            xt(2)
            first_layer(0, 4)
            second_layer(0, 3)
            xt(3)
            for s in range(PAIRS):
                for e in range(5 if s == 0 else 0, E):
                    first_layer(s, e)
                    if s == 0 and e == 5:
                        gate()
                    if e >= 1:
                        second_layer(s, e - 1)
                    else:
                        second_layer(s - 1, E - 1)
                    if s == 0 and e == 5:
                        turn_gates()
                    for n in range(MISC_USES * PAIRS):
                        if MISC_SLOT[n] == E * s + e:
                            if n % MISC_USES == 0:
                                tokens(n // MISC_USES)
                            else:
                                weights(n // MISC_USES, n % MISC_USES - 1)
            second_layer(PAIRS - 1, E - 1)


def kernel(x, L0_conv_w_qkv, L0_conv_w_dw, L0_conv_w_pw, L0_conv_w_proj, L0_conv_bn_gamma, L0_conv_bn_beta,
           L0_conv_bn_mean, L0_conv_bn_var, L0_ffn_Wg, L0_ffn_bg, L0_ffn_W1, L0_ffn_b1, L0_ffn_W2, L0_ffn_b2):
    import concourse.bacc as bacc
    from concourse.bass_utils import run_bass_kernel_spmd

    def a(v):
        return np.asarray(v)

    consts, select = constants()
    w_dw = a(L0_conv_w_dw).reshape(G, I, DY, DX).transpose(3, 1, 0, 2).reshape(DX * I, G * DY)
    arrays = {
        "x": a(x).reshape(2, B // 2, C, N).transpose(0, 2, 1, 3).reshape(2 * C, B // 2 * N),
        "w_qkv": a(L0_conv_w_qkv).T,
        "w_dw": np.concatenate([w_dw, np.zeros((LOW - DX * I, G * DY), np.float32), w_dw]),
        "w_pw": a(L0_conv_w_pw).transpose(2, 0, 1).reshape(I, G * I),
        "w_proj": a(L0_conv_w_proj).T,
        "vectors": np.concatenate([a(L0_conv_bn_gamma), a(L0_conv_bn_beta), a(L0_conv_bn_mean), a(L0_conv_bn_var),
                                   a(L0_ffn_bg)]),
        "wg": a(L0_ffn_Wg),
        "w1": a(L0_ffn_W1),
        "b1": a(L0_ffn_b1).reshape(E * KC, 128).T,
        "w2": a(L0_ffn_W2).reshape(E * KC, 128, C).transpose(1, 0, 2).reshape(128, E * KC * C),
        "b2": a(L0_ffn_b2).T,
        "consts": consts,
        "select": select,
    }
    arrays = {f"in_{k}_dram": np.ascontiguousarray(v) for k, v in arrays.items()}
    nc = bacc.Bacc("TRN2", target_bir_lowering=False, num_devices=1)
    args = [nc.dram_tensor(k, v.shape, mybir.dt.from_np(v.dtype), kind="ExternalInput").ap() for k, v in arrays.items()]
    args.append(nc.dram_tensor("out_0_dram", (B, C, H, W), F32, kind="ExternalOutput").ap())
    build(nc, *args)
    r = run_bass_kernel_spmd(nc, [arrays], core_ids=[0])
    return r.results[0]["out_0_dram"]
```
